# Optimizing a Trainium2 kernel written in Bass

```python
import numpy as np
import jax
import jax.numpy as jnp

def _softmax(x, axis=-1):
    return jax.nn.softmax(x, axis=axis)

def _gelu(x):
    return jax.nn.gelu(x, approximate=True)

def _silu(x):
    return jax.nn.silu(x)

def _sigmoid(x):
    return jax.nn.sigmoid(x)

def _layernorm(x, axis=-1, eps=1e-05):
    m = jnp.mean(x, axis=axis, keepdims=True)
    v = jnp.var(x, axis=axis, keepdims=True)
    return (x - m) / jnp.sqrt(v + eps)

def _scatter_add(tgt, idx, src, axis=0):
    return tgt.at[idx].add(src)

def _segment_sum(src, seg, n):
    return jax.ops.segment_sum(src, seg, n)
kernel_name = 'mk_adj_preln_d4_adj_r2_6fa247'

def setup_inputs(seed: int=0):
    np.random.seed(seed)
    _w = jnp.asarray

    def _rec_inputs():
        import jax
        import jax.numpy as jnp
        _gk = jax.random.key(seed)
        x = -7.109e-05 + 0.9999 * jax.random.normal(jax.random.fold_in(_gk, 1), (128, 64, 256), jnp.float32)
        _a = jax.random.bernoulli(jax.random.fold_in(_gk, 2), 0.125, (128, 64, 64))
        _a = jnp.logical_or(_a, jnp.swapaxes(_a, -1, -2))
        _a = jnp.logical_or(_a, jnp.eye(64, dtype=bool))
        adj = _a
        return (x, adj)
    x, adj = _rec_inputs()

    def _L0_gnn_setup():
        import jax, jax.numpy as jnp
        import numpy as np
        B, S, D, H = (1024, 64, 256, 8)
        HD = D // H
        SCALE = float(1.0 / np.sqrt(HD))

        def _static_masks():
            sq = np.arange(64)
            r = sq // 8
            f = sq % 8
            ri, rj = (r[:, None], r[None, :])
            fi, fj = (f[:, None], f[None, :])
            dr = np.abs(ri - rj)
            df = np.abs(fi - fj)
            eye = np.eye(64, dtype=bool)
            file_m = fi == fj
            rank_m = ri == rj
            diag_m = ri - fi == rj - fj
            adiag_m = ri + fi == rj + fj
            knight_m = (dr == 2) & (df == 1) | (dr == 1) & (df == 2) | eye
            king_m = (dr <= 1) & (df <= 1)
            return np.stack([file_m, rank_m, diag_m, adiag_m, knight_m, king_m])
        STATIC = jnp.asarray(_static_masks())
        EYE = jnp.eye(S, dtype=bool)
        key = jax.random.key(seed)
        ks = jax.random.split(key, 7)
        x = jax.random.normal(ks[0], (B, S, D), jnp.float32)
        ray_mask = jax.random.bernoulli(ks[1], 0.15, (B, S, S))
        attack_mask = jax.random.bernoulli(ks[2], 0.1, (B, S, S))
        s = 1.0 / np.sqrt(D)

        def lin(k):
            k1, k2 = jax.random.split(k)
            W = jax.random.uniform(k1, (D, D), jnp.float32, -s, s)
            b = jax.random.uniform(k2, (D,), jnp.float32, -s, s)
            return (W, b)
        Wq, bq = lin(ks[3])
        Wk, bk = lin(ks[4])
        Wv, bv = lin(ks[5])
        Wo, bo = lin(ks[6])
        return dict(x=x, ray_mask=ray_mask, attack_mask=attack_mask, Wq=Wq, bq=bq, Wk=Wk, bk=bk, Wv=Wv, bv=bv, Wo=Wo, bo=bo)
    _L0_gnn_all = _L0_gnn_setup()
    _L0_gnn_in = {k: v for k, v in _L0_gnn_all.items() if k in ('Wq', 'bq', 'Wk', 'bk', 'Wv', 'bv', 'Wo', 'bo')}
    del _L0_gnn_all

    def _L1_gnn_setup():
        import jax, jax.numpy as jnp
        import numpy as np
        QUERY_DIM = 256
        HEADS = 4
        DIM_HEAD = 64
        INNER = HEADS * DIM_HEAD
        B, N = (4, 1024)
        key = jax.random.key(seed)
        ks = jax.random.split(key, 6)
        s = 1.0 / np.sqrt(QUERY_DIM)
        x = jax.random.normal(ks[0], (B, N, QUERY_DIM), dtype=jnp.float32)
        adjacency_mask = jax.random.randint(ks[1], (B, N, N), 0, 2) > 0
        Wq = jax.random.normal(ks[2], (QUERY_DIM, INNER), dtype=jnp.float32) * s
        Wk = jax.random.normal(ks[3], (QUERY_DIM, INNER), dtype=jnp.float32) * s
        Wv = jax.random.normal(ks[4], (QUERY_DIM, INNER), dtype=jnp.float32) * s
        Wo = jax.random.normal(ks[5], (INNER, QUERY_DIM), dtype=jnp.float32) * (1.0 / np.sqrt(INNER))
        bo = jnp.zeros((QUERY_DIM,), dtype=jnp.float32)
        return {'x': x, 'adjacency_mask': adjacency_mask, 'Wq': Wq, 'Wk': Wk, 'Wv': Wv, 'Wo': Wo, 'bo': bo}
    _L1_gnn_all = _L1_gnn_setup()
    _L1_gnn_in = {k: v for k, v in _L1_gnn_all.items() if k in ('Wq', 'Wk', 'Wv', 'Wo', 'bo')}
    del _L1_gnn_all

    def _L2_gnn_setup():
        import jax, jax.numpy as jnp
        import numpy as np
        B, N, IN, OUT, H = (16, 512, 256, 256, 4)
        key = jax.random.key(seed)
        ks = jax.random.split(key, 10)
        s = 0.03
        return {'h': jax.random.normal(ks[0], (B, N, IN), jnp.float32), 'adj': jax.random.randint(ks[1], (B, N, N), 0, 2) > 0, 'W': jax.random.normal(ks[2], (H, OUT, IN), jnp.float32) * s, 'bW': jax.random.normal(ks[3], (H, OUT), jnp.float32) * s, 'attn': jax.random.normal(ks[4], (H, OUT, OUT), jnp.float32) * s, 'A_w': jax.random.normal(ks[5], (OUT, OUT * H), jnp.float32) * s, 'fc_w': jax.random.normal(ks[6], (OUT, IN), jnp.float32) * s, 'g1_w': jax.random.normal(ks[7], (OUT, OUT), jnp.float32) * s, 'g2_w': jax.random.normal(ks[8], (OUT, OUT), jnp.float32) * s, 'gbias': jax.random.normal(ks[9], (OUT,), jnp.float32) * s}
    _L2_gnn_all = _L2_gnn_setup()
    _L2_gnn_in = {k: v for k, v in _L2_gnn_all.items() if k in ('W', 'bW', 'attn', 'A_w', 'fc_w', 'g1_w', 'g2_w', 'gbias')}
    del _L2_gnn_all

    def _L3_gnn_setup():
        import jax, jax.numpy as jnp
        import numpy as np
        QUERY_DIM = 256
        HEADS = 4
        DIM_HEAD = 64
        INNER = HEADS * DIM_HEAD
        B, N = (4, 1024)
        key = jax.random.key(seed)
        ks = jax.random.split(key, 6)
        s = 1.0 / np.sqrt(QUERY_DIM)
        x = jax.random.normal(ks[0], (B, N, QUERY_DIM), dtype=jnp.float32)
        adjacency_mask = jax.random.randint(ks[1], (B, N, N), 0, 2) > 0
        Wq = jax.random.normal(ks[2], (QUERY_DIM, INNER), dtype=jnp.float32) * s
        Wk = jax.random.normal(ks[3], (QUERY_DIM, INNER), dtype=jnp.float32) * s
        Wv = jax.random.normal(ks[4], (QUERY_DIM, INNER), dtype=jnp.float32) * s
        Wo = jax.random.normal(ks[5], (INNER, QUERY_DIM), dtype=jnp.float32) * (1.0 / np.sqrt(INNER))
        bo = jnp.zeros((QUERY_DIM,), dtype=jnp.float32)
        return {'x': x, 'adjacency_mask': adjacency_mask, 'Wq': Wq, 'Wk': Wk, 'Wv': Wv, 'Wo': Wo, 'bo': bo}
    _L3_gnn_all = _L3_gnn_setup()
    _L3_gnn_in = {k: v for k, v in _L3_gnn_all.items() if k in ('Wq', 'Wk', 'Wv', 'Wo', 'bo')}
    del _L3_gnn_all
    return {'x': x, 'adj': adj, 'L0_gnn_Wq': _L0_gnn_in['Wq'], 'L0_gnn_bq': _L0_gnn_in['bq'], 'L0_gnn_Wk': _L0_gnn_in['Wk'], 'L0_gnn_bk': _L0_gnn_in['bk'], 'L0_gnn_Wv': _L0_gnn_in['Wv'], 'L0_gnn_bv': _L0_gnn_in['bv'], 'L0_gnn_Wo': _L0_gnn_in['Wo'], 'L0_gnn_bo': _L0_gnn_in['bo'], 'L1_gnn_Wq': _L1_gnn_in['Wq'], 'L1_gnn_Wk': _L1_gnn_in['Wk'], 'L1_gnn_Wv': _L1_gnn_in['Wv'], 'L1_gnn_Wo': _L1_gnn_in['Wo'], 'L1_gnn_bo': _L1_gnn_in['bo'], 'L2_gnn_W': _L2_gnn_in['W'], 'L2_gnn_bW': _L2_gnn_in['bW'], 'L2_gnn_attn': _L2_gnn_in['attn'], 'L2_gnn_A_w': _L2_gnn_in['A_w'], 'L2_gnn_fc_w': _L2_gnn_in['fc_w'], 'L2_gnn_g1_w': _L2_gnn_in['g1_w'], 'L2_gnn_g2_w': _L2_gnn_in['g2_w'], 'L2_gnn_gbias': _L2_gnn_in['gbias'], 'L3_gnn_Wq': _L3_gnn_in['Wq'], 'L3_gnn_Wk': _L3_gnn_in['Wk'], 'L3_gnn_Wv': _L3_gnn_in['Wv'], 'L3_gnn_Wo': _L3_gnn_in['Wo'], 'L3_gnn_bo': _L3_gnn_in['bo']}

def reference(x, adj, L0_gnn_Wq, L0_gnn_bq, L0_gnn_Wk, L0_gnn_bk, L0_gnn_Wv, L0_gnn_bv, L0_gnn_Wo, L0_gnn_bo, L1_gnn_Wq, L1_gnn_Wk, L1_gnn_Wv, L1_gnn_Wo, L1_gnn_bo, L2_gnn_W, L2_gnn_bW, L2_gnn_attn, L2_gnn_A_w, L2_gnn_fc_w, L2_gnn_g1_w, L2_gnn_g2_w, L2_gnn_gbias, L3_gnn_Wq, L3_gnn_Wk, L3_gnn_Wv, L3_gnn_Wo, L3_gnn_bo):
    import jax
    import jax.numpy as jnp

    def _L0_gnn_ref(x, ray_mask, attack_mask, Wq, bq, Wk, bk, Wv, bv, Wo, bo):
        import jax, jax.numpy as jnp
        import numpy as np
        B, S, D, H = (1024, 64, 256, 8)
        HD = D // H
        SCALE = float(1.0 / np.sqrt(HD))

        def _static_masks():
            sq = np.arange(64)
            r = sq // 8
            f = sq % 8
            ri, rj = (r[:, None], r[None, :])
            fi, fj = (f[:, None], f[None, :])
            dr = np.abs(ri - rj)
            df = np.abs(fi - fj)
            eye = np.eye(64, dtype=bool)
            file_m = fi == fj
            rank_m = ri == rj
            diag_m = ri - fi == rj - fj
            adiag_m = ri + fi == rj + fj
            knight_m = (dr == 2) & (df == 1) | (dr == 1) & (df == 2) | eye
            king_m = (dr <= 1) & (df <= 1)
            return np.stack([file_m, rank_m, diag_m, adiag_m, knight_m, king_m])
        STATIC = jnp.asarray(_static_masks())
        EYE = jnp.eye(S, dtype=bool)
        Bn = x.shape[0]

        def split_heads(t):
            return t.reshape(Bn, S, H, HD).transpose(0, 2, 1, 3)
        q = split_heads(x @ Wq.T + bq)
        k = split_heads(x @ Wk.T + bk)
        v = split_heads(x @ Wv.T + bv)
        scores = jnp.einsum('bhsd,bhtd->bhst', q, k) * SCALE
        mask = jnp.concatenate([jnp.broadcast_to(STATIC[None], (Bn, 6, S, S)), (ray_mask | EYE)[:, None], (attack_mask | EYE)[:, None]], axis=1)
        scores = jnp.where(mask, scores, jnp.float32(-1000000000.0))
        attn = jax.nn.softmax(scores, axis=-1)
        out = jnp.einsum('bhst,bhtd->bhsd', attn, v)
        out = out.transpose(0, 2, 1, 3).reshape(Bn, S, D)
        return out @ Wo.T + bo

    def _L1_gnn_ref(x, adjacency_mask, Wq, Wk, Wv, Wo, bo):
        import jax, jax.numpy as jnp
        import numpy as np
        QUERY_DIM = 256
        HEADS = 4
        DIM_HEAD = 64
        INNER = HEADS * DIM_HEAD
        B, N = (4, 1024)
        scale = DIM_HEAD ** (-0.5)

        def split_heads(t):
            b, n, _ = t.shape
            return t.reshape(b, n, HEADS, DIM_HEAD).transpose(0, 2, 1, 3)
        q = split_heads(x @ Wq)
        k = split_heads(x @ Wk)
        v = split_heads(x @ Wv)
        sim = jnp.einsum('bhid,bhjd->bhij', q, k) * scale
        neg = -jnp.finfo(sim.dtype).max
        sim = jnp.where(adjacency_mask[:, None, :, :], sim, neg)
        attn = jax.nn.softmax(sim, axis=-1)
        out = jnp.einsum('bhij,bhjd->bhid', attn, v)
        out = out.transpose(0, 2, 1, 3).reshape(x.shape[0], x.shape[1], INNER)
        return out @ Wo + bo

    def _L2_gnn_ref(h, adj, W, bW, attn, A_w, fc_w, g1_w, g2_w, gbias):
        import jax, jax.numpy as jnp
        import numpy as np
        B, N, IN, OUT, H = (16, 512, 256, 256, 4)
        Wh = jnp.einsum('bni,hoi->bhno', h, W) + bW[None, :, None, :]
        e = jnp.einsum('bhno,hop->bhnp', Wh, attn)
        scores = jnp.einsum('bhnp,bhmp->bhnm', e, Wh)
        A_mat = jnp.tanh(jnp.where(adj[:, None, :, :], scores, 0.0))
        hp = jax.nn.relu(jnp.einsum('bhnm,bhmo->bhno', A_mat, Wh))
        cat = jnp.transpose(hp, (0, 2, 1, 3)).reshape(hp.shape[0], hp.shape[2], -1)
        ha = cat @ A_w.T
        hf = h @ fc_w.T
        coeff = jax.nn.sigmoid(hf @ g1_w.T + ha @ g2_w.T + gbias)
        return hf * coeff + ha * (1.0 - coeff)

    def _L3_gnn_ref(x, adjacency_mask, Wq, Wk, Wv, Wo, bo):
        import jax, jax.numpy as jnp
        import numpy as np
        QUERY_DIM = 256
        HEADS = 4
        DIM_HEAD = 64
        INNER = HEADS * DIM_HEAD
        B, N = (4, 1024)
        scale = DIM_HEAD ** (-0.5)

        def split_heads(t):
            b, n, _ = t.shape
            return t.reshape(b, n, HEADS, DIM_HEAD).transpose(0, 2, 1, 3)
        q = split_heads(x @ Wq)
        k = split_heads(x @ Wk)
        v = split_heads(x @ Wv)
        sim = jnp.einsum('bhid,bhjd->bhij', q, k) * scale
        neg = -jnp.finfo(sim.dtype).max
        sim = jnp.where(adjacency_mask[:, None, :, :], sim, neg)
        attn = jax.nn.softmax(sim, axis=-1)
        out = jnp.einsum('bhij,bhjd->bhid', attn, v)
        out = out.transpose(0, 2, 1, 3).reshape(x.shape[0], x.shape[1], INNER)
        return out @ Wo + bo
    h = jnp.maximum(_layernorm(x, axis=-1), 0.0)
    x = x + _L0_gnn_ref(h, adj, adj, L0_gnn_Wq, L0_gnn_bq, L0_gnn_Wk, L0_gnn_bk, L0_gnn_Wv, L0_gnn_bv, L0_gnn_Wo, L0_gnn_bo)
    h = jnp.maximum(_layernorm(x, axis=-1), 0.0)
    x = x + _L1_gnn_ref(h, adj, L1_gnn_Wq, L1_gnn_Wk, L1_gnn_Wv, L1_gnn_Wo, L1_gnn_bo)
    h = jnp.maximum(_layernorm(x, axis=-1), 0.0)
    x = x + _L2_gnn_ref(h, adj, L2_gnn_W, L2_gnn_bW, L2_gnn_attn, L2_gnn_A_w, L2_gnn_fc_w, L2_gnn_g1_w, L2_gnn_g2_w, L2_gnn_gbias)
    h = jnp.maximum(_layernorm(x, axis=-1), 0.0)
    x = x + _L3_gnn_ref(h, adj, L3_gnn_Wq, L3_gnn_Wk, L3_gnn_Wv, L3_gnn_Wo, L3_gnn_bo)
    return x

_drawn_inputs = setup_inputs


def setup_inputs(seed=0):
    import zlib

    import numpy as np

    out = dict(_drawn_inputs(seed))
    spreads = {'L1_gnn_bo': (0.0, 0.1), 'L3_gnn_bo': (0.0, 0.1)}
    factors = {'L0_gnn_Wq': 6.91,
     'L0_gnn_bq': 8.0,
     'L0_gnn_Wk': 6.813,
     'L0_gnn_bk': 8.0,
     'L2_gnn_gbias': 8.0}
    for name, (base, spread) in spreads.items():
        noise = np.random.default_rng([zlib.crc32(name.encode()), seed]).standard_normal(out[name].shape)
        drawn = base * np.exp(spread * noise) if base else spread * noise
        out[name] = jnp.asarray(drawn.astype(out[name].dtype))
    for name, factor in factors.items():
        out[name] = (out[name] * factor).astype(out[name].dtype)
    return out
```

```python
from contextlib import ExitStack

import concourse.bass as bass
import numpy as np
from concourse import mybir

F32 = mybir.dt.float32
F32R = mybir.dt.float32r
BF16 = mybir.dt.bfloat16
U8 = mybir.dt.uint8
ALU = mybir.AluOpType
ACT = mybir.ActivationFunctionType
AX_X = mybir.AxisListType.X

P = 128
SQ = 64
D = 256
DC = D // P
NB = 4
TOK = NB * SQ
TT = TOK // P
H2 = 4
SLOTS = 2
EPS = 1e-5
MASKED = -1e30

ATT = [dict(layer=0, heads=8, mats=0, bias=1), dict(layer=1, heads=4, mats=4, bias=2),
       dict(layer=3, heads=4, mats=8, bias=3)]
M_G, M_W, M_A, M_FG, M_G2, MATS = 12, 16, 20, 24, 26, 27
R_WNAT, R_WT, R_ATT, R_AW, R_FCT, R_FCNAT, R_G1T, R_G2T, RAW = 12, 16, 20, 24, 28, 29, 30, 31, 32
C_ID, C_EYE, C_STATIC, C_ONES, C_SEL1, C_SEL2, C_SELAB, C_EPS, CST = 0, 128, 192, 384, 512, 640, 768, 770, 772

SPLITS = [(M_W, R_WT, 4), (0, 0, 4), (4, 4, 4), (8, 8, 4), (M_A, R_AW, 4), (M_FG, R_FCT, 1), (M_G2, R_G2T, 1)]


def constants():
    c = np.zeros((P, CST), np.float32)
    c[:, C_ID:C_ID + P] = np.eye(P)
    sq = np.arange(SQ)
    r, f = sq // 8, sq % 8
    dr, df = abs(r[:, None] - r[None]), abs(f[:, None] - f[None])
    eye = np.eye(SQ, dtype=bool)
    masks = [f[:, None] == f[None], r[:, None] == r[None],
             r[:, None] - f[:, None] == r[None] - f[None], r[:, None] + f[:, None] == r[None] + f[None],
             (dr == 2) & (df == 1) | (dr == 1) & (df == 2) | eye, (dr <= 1) & (df <= 1)]
    for half in range(2):
        rows = slice(SQ * half, SQ * half + SQ)
        c[rows, C_EYE:C_EYE + SQ] = np.where(eye, 0, MASKED)
        for pair in range(3):
            at = C_STATIC + SQ * pair
            c[rows, at:at + SQ] = np.where(masks[2 * pair + half], 0, MASKED)
    c[:, C_ONES + np.array([0, 1, 32])] = 1
    c[0:4, C_SEL1:C_SEL1 + P] = 0
    c[2:4, C_SEL1:C_SEL1 + P] = 1
    c[4:6, C_SEL2:C_SEL2 + P] = 1
    c[[0, 2, 4, 32], C_SELAB] = 1
    c[[1, 3, 5], C_SELAB + 1] = 1
    c[:, C_EPS] = EPS
    c[:, C_EPS + 1] = -0.5
    return c


class Counts:

    def __init__(self, i, keep=lambda x: x):
        self.once = keep(i + 1)
        self.two = [keep(i * 2 + (n + 1)) for n in range(2)]
        self.att = [keep(i * 3 + (n + 1)) for n in range(3)]
        self.four = [keep(i * 4 + (n + 1)) for n in range(4)]
        self.dma = keep(i * 16 + 16)
        self.dma2 = keep(i * 32 + 32)


def build(nc, x_in, adjq_in, adjt_in, mats_in, cols_in, rows_in, cst_in, out):
    GROUPS = x_in.shape[0] // TOK
    ITERS = GROUPS // SLOTS
    x_v = x_in.rearrange("(g t p) d -> p g t d", t=TT, p=P)
    out_v = out.rearrange("(g t p) d -> p g t d", t=TT, p=P)
    adjq_v = adjq_in.rearrange("q (g b) k -> q g (b k)", b=NB)
    adjt_v = adjt_in.rearrange("e k (g t) q -> e k g t q", t=TT)

    ctx = ExitStack()
    with ctx:
        def sb(name, shape, dt, scope=ctx):
            return scope.enter_context(nc.sbuf_tensor(name, shape, dt))

        def sem(name):
            return ctx.enter_context(nc.semaphore(name))

        WHI = sb("w_hi", [P, MATS, DC, D], F32R)
        WLO = sb("w_lo", [P, MATS, DC, D], F32R)
        ROWS = sb("bias_rows", [SQ, H2 * D], F32R)
        SELR = sb("sel_rows", [P, 3, P], F32R)
        CF = sb("consts", [P, P + SQ + 2], F32)
        ONES4 = sb("ones4", [H2, P], F32)
        STATIC = sb("static_masks", [P, 3, SQ], BF16)
        COLS = sb("bias_cols", [P, 12], F32)
        CVEC = sb("c_vec", [P, DC, H2], F32)
        UVEC = sb("u_vec", [P, DC, H2], F32)
        S0 = sb("s0", [H2, 1], F32)
        IDENT = CF[:, 0:P]
        EYE = CF[:, P:P + SQ]
        EPSC = CF[:, P + SQ:P + SQ + 2]

        X, XN, HT, MASKA, MASKO, ADJ8, ADJT8, SMALL = ([] for _ in range(8))
        for s in range(SLOTS):
            X.append(sb(f"x{s}", [P, TT * D], F32))
            XN.append(sb(f"xn{s}", [P, TT * D], F32))
            HT.append(sb(f"hT{s}", [P, 2, DC, TOK], F32R))
            MASKA.append(sb(f"mask_adj{s}", [P, TOK], BF16))
            MASKO.append(sb(f"mask_adj_eye{s}", [P, TOK], BF16))
            ADJ8.append(sb(f"adj8_{s}", [P, TOK], U8))
            ADJT8.append(sb(f"adjT8_{s}", [P, TT, 2, SQ], U8))
            SMALL.append(sb(f"small{s}", [P, 72], F32))
        STATS = [m[:, 0:12].rearrange("p (t c) -> p t c", t=TT) for m in SMALL]
        MV = [m[:, 12:16].rearrange("p (t c) -> p t c", t=TT) for m in SMALL]
        VE = [m[:, 16:18] for m in SMALL]
        RSTD = [m[:, 18:20] for m in SMALL]
        ROWMAX = [m[:, 20:36] for m in SMALL]
        ROWSUM = [m[:, 36:52] for m in SMALL]
        RECIP = [m[:, 52:68] for m in SMALL]

        scope = ExitStack()
        RAWM = sb("raw_mats", [P, RAW, DC, D], F32, scope)
        T1 = RAWM[:, 0:H2, :, :]
        RAWR = sb("raw_rows", [SQ, H2 * D], F32, scope)
        RAWRH = HT[0][0:SQ, :, :, :].rearrange("p j c k -> p (j c k)")
        RAWC = sb("raw_consts", [P, CST], F32, scope)
        A1 = sb("attn_b", [P, DC, H2], F32, scope)
        S0M = sb("s0_matrix", [H2, H2], F32, scope)
        scope.close()
        scope = ExitStack()
        Q, K, V, PR, PTS, OT = ([] for _ in range(6))
        for s in range(SLOTS):
            Q.append(sb(f"qT{s}", [P, DC, TOK], F32, scope))
            K.append(sb(f"kT{s}", [P, DC, TOK], F32, scope))
            V.append(sb(f"v{s}", [P, TT, D], F32, scope))
            PR.append(sb(f"probs{s}", [P, 2, 512], F32, scope))
            PTS.append(sb(f"probsT{s}", [P, 2, 512], F32, scope))
            OT.append(sb(f"oT{s}", [P, 2, DC, TOK], F32R, scope))
            sb(f"pad{s}", [P, 4608], F32, scope)
        scope.close()
        scope = ExitStack()
        WIDE, AT, F, RS, CT = ([] for _ in range(5))
        for s in range(SLOTS):
            WIDE.append(sb(f"wide{s}", [P, 2, DC, TOK * H2], F32R, scope))
            AT.append(sb(f"aT{s}", [P, 2, TT, 512], F32R, scope))
            F.append(sb(f"f{s}", [P, 1024], F32, scope))
            RS.append(sb(f"rs{s}", [SQ, TOK * H2], F32R, scope))
            CT.append(sb(f"cT{s}", [P, 2, 512], F32R, scope))
        scope.close()

        PS = ctx.enter_context(nc.psum_tensor("ps", [P, 8, 512], F32))

        def bank(s, n):
            return PS[:, 4 * s + n, :]

        def o_view(s):
            return PS[:, 4 * s + 2:4 * s + 4, 0:256].rearrange("p e (f q) -> p f e q", q=SQ)

        def e_view(s, part, oc, h):
            return WIDE[s][:, part, oc, :].rearrange("p (b h q) -> p b h q", h=H2, q=SQ)[:, :, h, :]

        def e_bank(s, b, oc):
            return bank(s, b)[:, oc * TOK:oc * TOK + TOK].rearrange("p (b q) -> p b q", q=SQ)

        def tanh_buf(s, t):
            return XN[s][:, :] if t == 0 else F[s][:, 0:512]

        ONCE = (["s1_ps", "pt1_ps", "pt1_sb", "r_ps", "r4_ready", "hh_ready", "hl_ready",
                 "ha_sb", "x_ha", "hat_ps", "hat_hi", "hat_lo", "res2"])
        TWICE = ["s2_ps", "tanh", "at_f", "at_hi", "at_lo", "rs_ps", "rs_hi", "rs_lo", "g_ps", "gate_t", "masks"]
        FOUR = ["e_ps", "e_hi", "e_lo", "ah_ps", "ah_hi", "ah_lo", "hp_ps", "ct_hi", "ct_lo", "ha_mm"]
        NORM = ["bn", "var", "ve", "rstd", "xn_ready", "hT_ps", "hT_hi", "hT_lo"]
        ATTS = ["q_ps", "k_ps", "v_ps", "q_sb", "k_sb", "v_sb", "s_ps", "masked", "rowmax", "shifted", "exp", "rowsum",
                "recip", "probs", "gate", "pt_ps", "pt_sb", "o_ps", "oT_hi", "oT_lo", "y_ps", "res"]
        S = [{n: sem(f"{n}_{s}") for n in ONCE + TWICE + FOUR + NORM + ATTS + ["x_in", "adj_in", "adjT_in", "stored"]}
             for s in range(SLOTS)]
        raw_sems = [sem(f"raw_in{n}") for n in range(2, RAW // 4)]
        cst_ready, setup = sem("consts_in"), {n: sem(n) for n in (
            "consts", "waited", "rows", "w_hi", "w_lo", "t1_ps", "t1_sb", "g_ps", "g_hi", "g_lo",
            "vec_ps", "vec_sb", "zeroed")}

        block = ctx.enter_context(nc.Block())

        STEPS = ([("att", 0, k) for k in range(6)] + [("att", 1, k) for k in range(6)]
                 + [("l2", 2, k) for k in range(6)] + [("att", 2, k) for k in range(6)])
        LAG = len(STEPS) // 2

        def passes(eng, step):
            n = len(STEPS)

            def turn(first, now, before):
                for k in range(n):
                    step(0, STEPS[k], now)
                    if k >= LAG:
                        step(1, STEPS[k - LAG], now)
                    elif not first:
                        step(1, STEPS[n - LAG + k], before)

            turn(True, Counts(0), None)
            if ITERS > 1:
                with eng.Fori(0, ITERS - 1) as i:
                    turn(False, Counts(i + 1, eng.snap), Counts(i, eng.snap))
            last = Counts(ITERS - 1)
            for k in range(n - LAG, n):
                step(1, STEPS[k], last)

        def alone(eng):
            eng.sem_inc(setup["waited"], 1)

        def norm_index(kind, which):
            return 2 if kind == "l2" else ATT[which]["layer"]

        @block.sync
        def _(sp):
            sp.dma_start(RAWC[:, :], cst_in).then_inc(cst_ready, 16)
            sp.dma_start(COLS[:, :], cols_in).then_inc(cst_ready, 16)
            sp.dma_start(RAWR[:, :], rows_in).then_inc(cst_ready, 16)
            for n in (4, 3, 5, 0, 1, 2, 6, 7):
                sp.dma_start(RAWM[:, 4 * n:4 * n + 4, :, :],
                             mats_in[4 * n:4 * n + 4, :, :].rearrange("m (c p) o -> p m c o", p=P)
                             ).then_inc(raw_sems[max(n - 2, 0)], 16)
            sp.wait_ge(setup["zeroed"], 1)

            def load_x(s, g):
                sp.dma_start(X[s][:, :].rearrange("p (t d) -> p t d", t=TT), x_v[:, g, :, :]).then_inc(S[s]["x_in"], 16)

            def load_adj(s, g):
                for half in range(2):
                    sp.dma_start(ADJ8[s][SQ * half:SQ * half + SQ, :], adjq_v[:, g, :]).then_inc(S[s]["adj_in"], 16)

            def load_adjT(s, g):
                for e in range(2):
                    sp.dma_start(ADJT8[s][SQ * e:SQ * e + SQ, :, e, :], adjt_v[e, :, g, :, :]
                                 ).then_inc(S[s]["adjT_in"], 16)

            for s in range(SLOTS):
                load_x(s, s)
                load_adj(s, s)
                load_adjT(s, s)

            def turn(s, g, gnext, now):
                if gnext is not None:
                    sp.wait_ge(S[s]["masks"], now.two[0])
                    alone(sp)
                    sp.wait_ge(S[s]["at_f"], now.two[1])
                    alone(sp)
                    load_adj(s, gnext)
                    load_adjT(s, gnext)
                sp.wait_ge(S[s]["res"], now.att[2])
                sp.dma_start(out_v[:, g, :, :], X[s][:, :].rearrange("p (t d) -> p t d", t=TT)
                             ).then_inc(S[s]["stored"], 16)
                if gnext is not None:
                    sp.wait_ge(S[s]["stored"], now.dma)
                    load_x(s, gnext)

            if ITERS > 1:
                with sp.Fori(0, ITERS - 1) as i:
                    now = Counts(i, sp.snap)
                    for s in range(SLOTS):
                        turn(s, sp.snap(i * SLOTS + s), sp.snap(i * SLOTS + SLOTS + s), now)
            for s in range(SLOTS):
                turn(s, GROUPS - SLOTS + s, None, Counts(ITERS - 1))
                sp.wait_ge(S[s]["stored"], 16 * ITERS)

        @block.gpsimd
        def _(pool):
            nc.gpsimd.memset(ONES4[:, :], 1.0)
            for s in range(SLOTS):
                last = nc.gpsimd.memset(ADJT8[s][:, :, :, :], 0.0)
            last.then_inc(setup["zeroed"], 1)

            def step(s, what, v):
                kind, which, k = what
                sm = S[s]
                if k == 0:
                    n = v.four[norm_index(kind, which)]
                    pool.wait_ge(sm["var"], n)
                    nc.gpsimd.tensor_tensor(VE[s], MV[s][:, :, 1], EPSC[:, 0:1].broadcast_to([P, TT]), ALU.add
                                            ).then_inc(sm["ve"], 1)
                    pool.wait_ge(sm["ve"], n)
                    nc.gpsimd.tensor_tensor(RSTD[s], VE[s], EPSC[:, 1:2].broadcast_to([P, TT]), ALU.pow
                                            ).then_inc(sm["rstd"], 1)
                elif kind == "l2" and k == 5:
                    pool.wait_ge(sm["ha_sb"], v.once)
                    nc.gpsimd.tensor_tensor(X[s][:, :], X[s][:, :], F[s][:, 0:512], ALU.add).then_inc(sm["x_ha"], 1)

            pool.wait_ge(setup["consts"], 1)
            passes(pool, step)

        @block.tensor
        def _(pe):
            def mm(o, lhsT, rhs, start, stop):
                return nc.tensor.matmul(o, lhsT, rhs, start=start, stop=stop, skip_group_check=True)

            def split3(o, terms, start=True, stop=True):
                n = 3 * len(terms)
                i = 0
                for lh, ll, rh, rl in terms:
                    for a, b in ((lh, rh), (lh, rl), (ll, rh)):
                        last = mm(o, a, b, start and i == 0, stop and i == n - 1)
                        i += 1
                return last

            bcol = COLS[:, 4:12].rearrange("p (h c) -> p h c", h=H2)
            pe.wait_ge(setup["consts"], 1)
            pe.wait_ge(raw_sems[1], 16)
            pe.wait_ge(raw_sems[3], 16)
            for h in range(H2):
                for oc in range(DC):
                    for c in range(DC):
                        last = mm(PS[:, h, oc * D:oc * D + D], RAWM[:, R_ATT + h, c, oc * P:oc * P + P],
                                  RAWM[:, R_WNAT + h, c, :], c == 0, c == DC - 1)
                last.then_inc(setup["t1_ps"], 1)
            for h in range(H2):
                for oc in range(DC):
                    for c in range(DC):
                        last = mm(PS[:, 4, oc * H2 + h:oc * H2 + h + 1], RAWM[:, R_ATT + h, c, oc * P:oc * P + P],
                                  bcol[:, h, c:c + 1], c == 0, c == DC - 1)
            last.then_inc(setup["vec_ps"], 1)
            pe.wait_ge(setup["t1_sb"], H2)
            for h in range(H2):
                for ic in range(DC):
                    for c in range(DC):
                        last = mm(PS[:, h, ic * D:ic * D + D], RAWM[:, R_WNAT + h, c, ic * P:ic * P + P],
                                  T1[:, h, c, :], c == 0, c == DC - 1)
                last.then_inc(setup["g_ps"], 1)
            pe.wait_ge(raw_sems[5], 16)
            for ic in range(DC):
                for c in range(DC):
                    last = mm(PS[:, 5, ic * D:ic * D + D], RAWM[:, R_FCNAT, c, ic * P:ic * P + P],
                              RAWM[:, R_G1T, c, :], c == 0, c == DC - 1)
            last.then_inc(setup["g_ps"], 1)
            pe.wait_ge(setup["vec_sb"], 1)
            for h in range(H2):
                for ic in range(DC):
                    for c in range(DC):
                        at = ic * H2 + h
                        mm(PS[:, 6, at:at + 1], T1[:, h, c, ic * P:ic * P + P], bcol[:, h, c:c + 1],
                           c == 0, c == DC - 1)
                        mm(PS[:, 7, at:at + 1], RAWM[:, R_WNAT + h, c, ic * P:ic * P + P], A1[:, c, h:h + 1],
                           c == 0, c == DC - 1)
            for c in range(DC):
                last = mm(PS[0:H2, 4, 0:H2], bcol[:, :, c], A1[:, c, :], c == 0, c == DC - 1)
            last.then_inc(setup["vec_ps"], 1)
            pe.wait_ge(setup["consts"], 2)
            pe.wait_ge(setup["zeroed"], 1)
            pe.wait_ge(setup["w_lo"], len(SPLITS))
            pe.wait_ge(setup["g_lo"], H2 + 1)
            pe.wait_ge(setup["vec_sb"], 3)
            pe.wait_ge(setup["rows"], 4)

            def transposed_h(s, n):
                sm = S[s]
                pe.wait_ge(sm["xn_ready"], n)
                for c in range(DC):
                    for t in range(TT):
                        last = nc.tensor.transpose(bank(s, 0)[:, c * TOK + t * P:c * TOK + t * P + P],
                                                   XN[s][:, t * D + c * P:t * D + c * P + P], IDENT)
                last.then_inc(sm["hT_ps"], 1)

            def features_out(s, o, m, oc):
                return split3(o, [(WHI[:, m, c, oc * P:oc * P + P], WLO[:, m, c, oc * P:oc * P + P],
                                   HT[s][:, 0, c, :], HT[s][:, 1, c, :]) for c in range(DC)])

            def tokens_out(o, actT, t, m, bias=None, start=True):
                last = split3(o, [(actT(0, c)[:, t * P:t * P + P], actT(1, c)[:, t * P:t * P + P],
                                   WHI[:, m, c, :], WLO[:, m, c, :]) for c in range(DC)],
                              start=start, stop=bias is None)
                if bias is not None:
                    last = mm(o, SELR[0:SQ, 1, :], ROWS[:, bias * D:bias * D + D], False, True)
                return last

            def att(s, a, k, v):
                sm, L, n = S[s], ATT[a], v.att[a]
                hd = D // L["heads"]
                two = L["heads"] == 8
                if k == 0:
                    transposed_h(s, v.four[L["layer"]])
                elif k == 1:
                    pe.wait_ge(sm["hT_lo"], v.four[L["layer"]])
                    for name, b, m in (("q_ps", 1, 0), ("k_ps", 2, 1)):
                        for oc in range(DC):
                            last = features_out(s, bank(s, b)[:, oc * TOK:oc * TOK + TOK], L["mats"] + m, oc)
                        last.then_inc(sm[name], 1)
                    for t in range(TT):
                        last = tokens_out(bank(s, 3)[:, t * D:t * D + D], lambda j, c: HT[s][:, j, c, :], t,
                                          L["mats"] + 2, 0 if a == 0 else None)
                    last.then_inc(sm["v_ps"], 1)
                elif k == 2:
                    pe.wait_ge(sm["q_sb"], n)
                    pe.wait_ge(sm["k_sb"], n)
                    alone(pe)
                    banks = 2 if two else 1
                    for j in range(banks):
                        for cj in range(2):
                            for b in range(NB):
                                for half in range(2):
                                    h = 2 * (j + banks * cj) + half
                                    r, c = h * hd % P, h * hd // P
                                    at = (cj * NB + b) * SQ
                                    last = mm(bank(s, j)[SQ * half:SQ * half + SQ, at:at + SQ],
                                              Q[s][r:r + hd, c, b * SQ:b * SQ + SQ],
                                              K[s][r:r + hd, c, b * SQ:b * SQ + SQ], True, True)
                        last.then_inc(sm["s1_ps" if j else "s_ps"], 1)
                elif k == 3:
                    pe.wait_ge(sm["probs"], n)
                    for j in range(2 if two else 1):
                        for at in range(0, 512, P):
                            last = nc.tensor.transpose(bank(s, 1 - j)[:, at:at + P], PR[s][:, j, at:at + P], IDENT)
                        last.then_inc(sm["pt1_ps" if j else "pt_ps"], 1)
                elif k == 4:
                    pe.wait_ge(sm["v_sb"], n)
                    pe.wait_ge(sm["pt_sb"], n)
                    if two:
                        pe.wait_ge(sm["pt1_sb"], v.once)
                    alone(pe)
                    for h in range(L["heads"]):
                        r, c = h * hd % P, h * hd // P
                        half, banks = h % 2, 2 if two else 1
                        j, cj = h // 2 % banks, h // 2 // banks
                        for t in range(TT):
                            for e in range(2):
                                at = cj * 256 + t * P + half * SQ
                                last = mm(bank(s, 2 + e)[r:r + hd, (c * TT + t) * SQ:(c * TT + t) * SQ + SQ],
                                          V[s][SQ * e:SQ * e + SQ, t, h * hd:h * hd + hd],
                                          PTS[s][SQ * e:SQ * e + SQ, j, at:at + SQ], True, True)
                    last.then_inc(sm["o_ps"], 1)
                else:
                    pe.wait_ge(sm["oT_lo"], n)
                    for t in range(TT):
                        last = tokens_out(bank(s, 0)[:, t * D:t * D + D], lambda j, c: OT[s][:, j, c, :], t,
                                          L["mats"] + 3, L["bias"])
                    last.then_inc(sm["y_ps"], 1)

            def l2(s, k, v):
                sm, n = S[s], v.once
                wide = lambda j, c: WIDE[s][:, j, c, :]
                ct = lambda h: (CT[s][:, 0, :], CT[s][:, 1, :]) if h % 2 == 0 else (AT[s][:, 0, 0, :], AT[s][:, 1, 0, :])
                if k == 0:
                    transposed_h(s, v.four[2])
                elif k == 1:
                    pe.wait_ge(sm["hT_lo"], v.four[2])
                    for j in range(2):
                        for c in range(DC):
                            last = mm(bank(s, 1)[0:H2, 0:TOK], UVEC[:, c, :], HT[s][:, j, c, :].bitcast(F32),
                                      j == 0 and c == 0, j == 1 and c == DC - 1)
                    last.then_inc(sm["r_ps"], 1)
                    for h, b in enumerate((2, 3, 0, 1)):
                        if h == 3:
                            pe.wait_ge(sm["r4_ready"], n)
                        for oc in range(DC):
                            last = features_out(s, bank(s, b)[:, oc * TOK:oc * TOK + TOK], M_G + h, oc)
                        last.then_inc(sm["e_ps"], 1)
                elif k == 2:
                    pe.wait_ge(sm["e_lo"], v.four[3])
                    for t in range(TT):
                        o = bank(s, 2 + t)
                        split3(o, [(HT[s][:, 0, c, t * P:t * P + P], HT[s][:, 1, c, t * P:t * P + P],
                                    wide(0, c)[:, t * 512:t * 512 + 512], wide(1, c)[:, t * 512:t * 512 + 512])
                                   for c in range(DC)], stop=False)
                        mm(o, ONES4[:, :], F[s][0:H2, t * 512:t * 512 + 512], False, True).then_inc(sm["s2_ps"], 1)
                elif k == 3:
                    for t in range(TT):
                        pe.wait_ge(sm["at_lo"], v.two[t])
                        for j in range(2):
                            last = mm(bank(s, t), SELR[:, 0, :], AT[s][:, j, t, :], j == 0, j == 1)
                        last.then_inc(sm["rs_ps"], 1)
                    for t in range(TT):
                        for c in range(DC):
                            if t:
                                pe.wait_ge(sm["rs_lo"], v.two[c])
                            at = t * D + c * P
                            split3(bank(s, 2 * (1 - t) + c), [(CT[s][:, 0, at:at + P], CT[s][:, 1, at:at + P],
                                                               AT[s][:, 0, t, :], AT[s][:, 1, t, :])]
                                   ).then_inc(sm["ah_ps"], 1)
                elif k == 4:
                    def hp(h):
                        for oc in range(DC):
                            o = bank(s, h % 2)[:, oc * TOK:oc * TOK + TOK]
                            part = lambda x: x.rearrange("p (b h q) -> p b h q", h=H2, q=SQ)[:, :, h, :]
                            split3(o, [(WHI[:, M_W + h, c, oc * P:oc * P + P], WLO[:, M_W + h, c, oc * P:oc * P + P],
                                        part(wide(0, c)), part(wide(1, c))) for c in range(DC)], stop=False)
                            last = mm(o, ROWS[:, h * D + oc * P:h * D + oc * P + P], part(RS[s][:, :]), False, True)
                        last.then_inc(sm["hp_ps"], 1)

                    def ha(h):
                        pe.wait_ge(sm["ct_lo"], v.four[h])
                        hi, lo = ct(h)
                        for t in range(TT):
                            for c in range(DC):
                                at = c * TOK + t * P
                                m = M_A + h
                                for i, (x, w) in enumerate(((hi, WHI), (hi, WLO), (lo, WHI))):
                                    last = mm(bank(s, 2)[:, t * D:t * D + D], x[:, at:at + P], w[:, m, c, :],
                                              h == 0 and t == 0 and c == 0 and i == 0,
                                              h == H2 - 1 and t == TT - 1 and c == DC - 1 and i == 2)
                        last.then_inc(sm["ha_mm"], 1)

                    pe.wait_ge(sm["ah_lo"], v.four[3])
                    hp(0)
                    hp(1)
                    for h in range(H2):
                        ha(h)
                        if h + 2 < H2:
                            hp(h + 2)
                else:
                    banks = (3, 1)
                    for t in range(TT):
                        o = bank(s, banks[t])
                        split3(o, [(HT[s][:, 0, c, t * P:t * P + P], HT[s][:, 1, c, t * P:t * P + P],
                                    WHI[:, M_FG:M_FG + 2, c, :], WLO[:, M_FG:M_FG + 2, c, :]) for c in range(DC)],
                               stop=False)
                        mm(o[:, D:2 * D], SELR[0:SQ, 2, :], ROWS[:, 0:D], False, False)
                    pe.wait_ge(sm["ha_sb"], n)
                    for c in range(DC):
                        for t in range(TT):
                            last = nc.tensor.transpose(bank(s, 0)[:, c * TOK + t * P:c * TOK + t * P + P],
                                                       F[s][:, t * D + c * P:t * D + c * P + P], IDENT)
                    last.then_inc(sm["hat_ps"], 1)
                    pe.wait_ge(sm["hat_lo"], n)
                    for t in range(TT):
                        tokens_out(bank(s, banks[t])[:, D:2 * D], lambda j, c: CT[s][:, j, c * TOK:c * TOK + TOK], t,
                                   M_G2, start=False).then_inc(sm["g_ps"], 1)

            def step(s, what, v):
                kind, which, k = what
                if kind == "att":
                    att(s, which, k, v)
                else:
                    l2(s, k, v)

            passes(pe, step)

        @block.scalar
        def _(act):
            fn = nc.scalar.activation
            act.wait_ge(cst_ready, 48)
            fn(CF[:, 0:P + SQ], RAWC[:, C_ID:C_ID + P + SQ], ACT.Copy)
            fn(CF[:, P + SQ:P + SQ + 2], RAWC[:, C_EPS:C_EPS + 2], ACT.Copy).then_inc(setup["consts"], 1)
            fn(STATIC[:, :, :], RAWC[:, C_STATIC:C_STATIC + 3 * SQ], ACT.Copy)
            fn(SELR[:, :, :], RAWC[:, C_ONES:C_ONES + 3 * P], ACT.Copy).then_inc(setup["consts"], 1)
            fn(RAWRH[:, :], RAWR[:, :], ACT.Copy).then_inc(setup["rows"], 1)
            for n, (m, r, k) in enumerate(SPLITS):
                act.wait_ge(raw_sems[max(r // 4 - 2, 0)], 48 if r < R_WNAT else 16)
                fn(WHI[:, m:m + k, :, :], RAWM[:, r:r + k, :, :], ACT.Copy).then_inc(setup["w_hi"], 1)
            act.wait_ge(setup["w_lo"], 2)
            for h in range(H2):
                act.wait_ge(setup["t1_ps"], h + 1)
                fn(T1[:, h, :, :], PS[:, h, :], ACT.Copy).then_inc(setup["t1_sb"], 1)
            for n in range(H2 + 1):
                act.wait_ge(setup["g_ps"], n + 1)
                m, b = (M_G + n, n) if n < H2 else (M_FG + 1, 5)
                fn(WHI[:, m, :, :], PS[:, b, :], ACT.Copy).then_inc(setup["g_hi"], 1)

            def att(s, a, k, v):
                sm, L, n = S[s], ATT[a], v.att[a]
                two = L["heads"] == 8
                if k == 0:
                    act.wait_ge(sm["hT_ps"], v.four[L["layer"]])
                    fn(HT[s][:, 0, :, :], bank(s, 0), ACT.Relu).then_inc(sm["hT_hi"], 1)
                elif k == 1:
                    act.wait_ge(sm["q_ps"], n)
                    if a == 0:
                        for oc in range(DC):
                            last = fn(Q[s][:, oc, :], bank(s, 1)[:, oc * TOK:oc * TOK + TOK], ACT.Identity,
                                      bias=COLS[:, oc:oc + 1])
                    else:
                        last = fn(Q[s][:, :, :], bank(s, 1), ACT.Copy)
                    last.then_inc(sm["q_sb"], 1)
                    act.wait_ge(sm["v_ps"], n)
                    fn(V[s][:, :, :], bank(s, 3), ACT.Copy).then_inc(sm["v_sb"], 1)
                elif k == 2:
                    act.wait_ge(sm["shifted"], n)
                    p = PR[s][:, :, :] if two else PR[s][:, 0, :]
                    fn(p, p, ACT.Exp).then_inc(sm["exp"], 1)
                elif k == 3:
                    act.wait_ge(sm["pt_ps"], n)
                    fn(PTS[s][:, 0, :], bank(s, 1), ACT.Copy).then_inc(sm["pt_sb"], 1)
                    if two:
                        act.wait_ge(sm["pt1_ps"], v.once)
                        fn(PTS[s][:, 1, :], bank(s, 0), ACT.Copy).then_inc(sm["pt1_sb"], 1)
                elif k == 4:
                    act.wait_ge(sm["o_ps"], n)
                    fn(OT[s][:, 0, :, :].rearrange("p c (t e q) -> p (c t) e q", t=TT, e=2), o_view(s), ACT.Copy
                       ).then_inc(sm["oT_hi"], 1)

            def l2(s, k, v):
                sm, n = S[s], v.once
                if k == 0:
                    act.wait_ge(sm["hT_ps"], v.four[2])
                    fn(HT[s][:, 0, :, :], bank(s, 0), ACT.Relu).then_inc(sm["hT_hi"], 1)
                    fn(CT[s][:, 0, :], XN[s][:, :], ACT.Relu).then_inc(sm["hh_ready"], 1)
                elif k == 1:
                    for h, b in enumerate((2, 3, 0, 1)):
                        act.wait_ge(sm["e_ps"], v.four[h])
                        for oc in range(DC):
                            last = fn(e_view(s, 0, oc, h), e_bank(s, b, oc), ACT.Identity, bias=CVEC[:, oc, h:h + 1])
                        last.then_inc(sm["e_hi"], 1)
                elif k == 2:
                    act.wait_ge(sm["hl_ready"], n)
                    for t in range(TT):
                        act.wait_ge(sm["s2_ps"], v.two[t])
                        fn(tanh_buf(s, t), bank(s, 2 + t), ACT.Tanh).then_inc(sm["tanh"], 1)
                    for t in range(TT):
                        act.wait_ge(sm["at_f"], v.two[t])
                        fn(AT[s][:, 0, t, :], tanh_buf(s, t), ACT.Copy).then_inc(sm["at_hi"], 1)
                elif k == 3:
                    for t in range(TT):
                        act.wait_ge(sm["rs_ps"], v.two[t])
                        fn(RS[s][:, t * 512:t * 512 + 512], bank(s, t)[0:SQ, :], ACT.Copy).then_inc(sm["rs_hi"], 1)
                    for i in range(4):
                        t, c = i // 2, i % 2
                        act.wait_ge(sm["ah_ps"], v.four[i])
                        fn(WIDE[s][:, 0, c, t * 512:t * 512 + 512], bank(s, 2 * (1 - t) + c), ACT.Copy
                           ).then_inc(sm["ah_hi"], 1)
                elif k == 4:
                    for h in range(H2):
                        act.wait_ge(sm["hp_ps"], v.four[h])
                        if h >= 2:
                            act.wait_ge(sm["ha_mm"], v.four[h - 2])
                        fn(CT[s][:, 0, :] if h % 2 == 0 else AT[s][:, 0, 0, :], bank(s, h % 2), ACT.Relu
                           ).then_inc(sm["ct_hi"], 1)
                    act.wait_ge(sm["ha_mm"], v.four[3])
                    fn(F[s][:, 0:512], bank(s, 2), ACT.Copy).then_inc(sm["ha_sb"], 1)
                else:
                    act.wait_ge(sm["hat_ps"], n)
                    fn(CT[s][:, 0, :], bank(s, 0), ACT.Copy).then_inc(sm["hat_hi"], 1)
                    for t, b in enumerate((3, 1)):
                        act.wait_ge(sm["g_ps"], v.two[t])
                        fn(XN[s][:, t * D:t * D + D], bank(s, b)[:, D:2 * D], ACT.Tanh, scale=0.5
                           ).then_inc(sm["gate_t"], 1)

            def step(s, what, v):
                kind, which, k = what
                if kind == "att":
                    att(s, which, k, v)
                else:
                    l2(s, k, v)

            passes(act, step)

        @block.vector
        def _(dve):
            tt, ts, stt = nc.vector.tensor_tensor, nc.vector.tensor_scalar, nc.vector.scalar_tensor_tensor

            def lo_part(o, full, hi):
                return tt(o, full, hi.bitcast(F32), ALU.subtract)

            dve.wait_ge(setup["rows"], 1)
            tt(RAWR[:, :], RAWR[:, :], RAWRH[:, :].bitcast(F32), ALU.subtract).then_inc(setup["rows"], 1)
            dve.wait_ge(setup["rows"], 2)
            ts(RAWR[:, :], RAWR[:, :], RAWC[0:SQ, C_SELAB + 1:C_SELAB + 2], None, ALU.mult).then_inc(setup["rows"], 1)
            dve.wait_ge(setup["rows"], 3)
            stt(ROWS[:, :], RAWRH[:, :].bitcast(F32), RAWC[0:SQ, C_SELAB:C_SELAB + 1], RAWR[:, :], ALU.mult, ALU.add
                ).then_inc(setup["rows"], 1)
            for n, (m, r, k) in enumerate(SPLITS):
                dve.wait_ge(setup["w_hi"], n + 1)
                lo_part(WLO[:, m:m + k, :, :], RAWM[:, r:r + k, :, :], WHI[:, m:m + k, :, :]).then_inc(setup["w_lo"], 1)
            dve.wait_ge(setup["vec_ps"], 1)
            nc.vector.tensor_copy(A1[:, :, :], PS[:, 4, 0:DC * H2]).then_inc(setup["vec_sb"], 1)
            for n in range(H2 + 1):
                dve.wait_ge(setup["g_hi"], n + 1)
                m, b = (M_G + n, n) if n < H2 else (M_FG + 1, 5)
                lo_part(WLO[:, m, :, :], PS[:, b, :].rearrange("p (c o) -> p c o", c=DC), WHI[:, m, :, :]
                        ).then_inc(setup["g_lo"], 1)
            dve.wait_ge(setup["vec_ps"], 2)
            nc.vector.tensor_copy(CVEC[:, :, :], PS[:, 6, 0:DC * H2])
            nc.vector.tensor_copy(UVEC[:, :, :], PS[:, 7, 0:DC * H2])
            tt(S0M[:, :], PS[0:H2, 4, 0:H2], IDENT[0:H2, 0:H2], ALU.mult).then_inc(setup["vec_sb"], 1)
            dve.wait_ge(setup["vec_sb"], 2)
            nc.vector.reduce_sum(S0[:, :], S0M[:, :], AX_X).then_inc(setup["vec_sb"], 1)
            dve.wait_ge(setup["vec_sb"], 3)

            def residual_before(s, kind, which, v):
                sm = S[s]
                if kind == "l2":
                    dve.wait_ge(sm["res"], v.att[1])
                elif which == 0:
                    dve.wait_ge(sm["x_in"], v.dma)
                elif which == 1:
                    dve.wait_ge(sm["res"], v.att[0])
                else:
                    dve.wait_ge(sm["res2"], v.once)

            def norm(s, kind, which, v):
                sm, n = S[s], v.four[norm_index(kind, which)]
                residual_before(s, kind, which, v)
                for t in range(TT):
                    last = nc.vector.bn_stats(STATS[s][:, t, :], X[s][:, t * D:t * D + D])
                last.then_inc(sm["bn"], 1)
                dve.wait_ge(sm["bn"], n)
                alone(dve)
                for t in range(TT):
                    last = nc.vector.bn_aggr(MV[s][:, t, :], STATS[s][:, t, :])
                last.then_inc(sm["var"], 1)
                if (kind, which) == ("att", 0):
                    masks(s, v)
                dve.wait_ge(sm["rstd"], n)
                for t in range(TT):
                    last = ts(XN[s][:, t * D:t * D + D], X[s][:, t * D:t * D + D], MV[s][:, t, 0:1],
                              RSTD[s][:, t:t + 1], ALU.subtract, ALU.mult)
                last.then_inc(sm["xn_ready"], 1)

            def masks(s, v):
                sm = S[s]
                dve.wait_ge(sm["adj_in"], v.dma2)
                ts(MASKA[s][:, :], ADJ8[s][:, :], -1.0, -MASKED, ALU.add, ALU.mult).then_inc(sm["masks"], 1)
                dve.wait_ge(sm["masks"], v.two[0])
                tt(MASKO[s][:, :].rearrange("p (b k) -> p b k", b=NB), MASKA[s][:, :].rearrange("p (b k) -> p b k", b=NB),
                   EYE.unsqueeze(1).broadcast_to([P, NB, SQ]), ALU.max).then_inc(sm["masks"], 1)

            def h_lo(s, n):
                dve.wait_ge(S[s]["hT_hi"], n)
                stt(HT[s][:, 1, :, :], bank(s, 0).rearrange("p (c k) -> p c k", c=DC), 0.0,
                    HT[s][:, 0, :, :].bitcast(F32), ALU.max, ALU.subtract).then_inc(S[s]["hT_lo"], 1)

            def att(s, a, k, v):
                sm, L, n = S[s], ATT[a], v.att[a]
                hd = D // L["heads"]
                two = L["heads"] == 8
                scale = float(hd) ** -0.5
                if k == 0:
                    norm(s, "att", a, v)
                    h_lo(s, v.four[L["layer"]])
                elif k == 1:
                    dve.wait_ge(sm["k_ps"], n)
                    if a == 0:
                        for oc in range(DC):
                            last = ts(K[s][:, oc, :], bank(s, 2)[:, oc * TOK:oc * TOK + TOK], COLS[:, 2 + oc:3 + oc],
                                      None, ALU.add)
                    else:
                        last = nc.vector.tensor_copy(K[s][:, :, :], bank(s, 2))
                    last.then_inc(sm["k_sb"], 1)
                elif k == 2:
                    boards = lambda x: x.rearrange("p (b k) -> p b k", k=SQ)

                    def masked(j, cj, mask):
                        at = slice(cj * TOK, cj * TOK + TOK)
                        return stt(boards(PR[s][:, j, at]), boards(bank(s, j)[:, at]), scale, mask, ALU.mult, ALU.add)

                    fixed = lambda pair: STATIC[:, pair:pair + 1, :].broadcast_to([P, NB, SQ])
                    dve.wait_ge(sm["s_ps"], n)
                    if two:
                        masked(0, 0, fixed(0))
                        masked(0, 1, fixed(2))
                        dve.wait_ge(sm["s1_ps"], v.once)
                        dve.wait_ge(sm["masks"], v.two[1])
                        masked(1, 0, fixed(1))
                        last = masked(1, 1, boards(MASKO[s][:, :]))
                    else:
                        pairs = lambda x: x.rearrange("p (c k) -> p c k", c=2)
                        last = stt(pairs(PR[s][:, 0, :]), pairs(bank(s, 0)), scale,
                                   MASKA[s][:, :].unsqueeze(1).broadcast_to([P, 2, TOK]), ALU.mult, ALU.add)
                    last.then_inc(sm["masked"], 1)
                    rows = 16 if two else 8
                    p = (PR[s][:, :, :] if two else PR[s][:, 0:1, :]).rearrange("p j (r k) -> p (j r) k", k=SQ)
                    each = lambda m: m[s][:, 0:rows].unsqueeze(2).broadcast_to([P, rows, SQ])
                    dve.wait_ge(sm["masked"], n)
                    nc.vector.reduce_max(ROWMAX[s][:, 0:rows], p, AX_X).then_inc(sm["rowmax"], 1)
                    dve.wait_ge(sm["rowmax"], n)
                    tt(p, p, each(ROWMAX), ALU.subtract).then_inc(sm["shifted"], 1)
                    dve.wait_ge(sm["exp"], n)
                    nc.vector.reduce_sum(ROWSUM[s][:, 0:rows], p, AX_X).then_inc(sm["rowsum"], 1)
                    dve.wait_ge(sm["rowsum"], n)
                    nc.vector.reciprocal(RECIP[s][:, 0:rows], ROWSUM[s][:, 0:rows]).then_inc(sm["recip"], 1)
                    dve.wait_ge(sm["recip"], n)
                    tt(p, p, each(RECIP), ALU.mult).then_inc(sm["probs"], 1)
                elif k == 4:
                    dve.wait_ge(sm["oT_hi"], n)
                    order = lambda x: x.rearrange("p c (t e q) -> p (c t) e q", t=TT, e=2)
                    lo_part(order(OT[s][:, 1, :, :]), o_view(s), order(OT[s][:, 0, :, :])).then_inc(sm["oT_lo"], 1)
                elif k == 5:
                    dve.wait_ge(sm["y_ps"], n)
                    tt(X[s][:, :], bank(s, 0), X[s][:, :], ALU.add).then_inc(sm["res"], 1)

            def l2(s, k, v):
                sm, n = S[s], v.once
                if k == 0:
                    norm(s, "l2", 2, v)
                    h_lo(s, v.four[2])
                    dve.wait_ge(sm["hh_ready"], n)
                    stt(CT[s][:, 1, :], XN[s][:, :], 0.0, CT[s][:, 0, :].bitcast(F32), ALU.max, ALU.subtract
                        ).then_inc(sm["hl_ready"], 1)
                elif k == 1:
                    dve.wait_ge(sm["r_ps"], n)
                    for h in range(H2):
                        last = ts(F[s][0:H2, :].rearrange("p (b h q) -> p b h q", h=H2, q=SQ)[:, :, h, :],
                                  bank(s, 1)[0:H2, 0:TOK].rearrange("p (b q) -> p b q", q=SQ), S0[:, :],
                                  IDENT[0:H2, h:h + 1], ALU.add, ALU.mult)
                    last.then_inc(sm["r4_ready"], 1)
                    for h, b in enumerate((2, 3, 0, 1)):
                        dve.wait_ge(sm["e_hi"], v.four[h])
                        for oc in range(DC):
                            last = stt(e_view(s, 1, oc, h), e_bank(s, b, oc), CVEC[:, oc, h:h + 1],
                                       e_view(s, 0, oc, h).bitcast(F32), ALU.add, ALU.subtract)
                        last.then_inc(sm["e_lo"], 1)
                elif k == 2:
                    dve.wait_ge(sm["adjT_in"], v.dma2)
                    for t in range(TT):
                        dve.wait_ge(sm["tanh"], v.two[t])
                        seen = ADJT8[s][:, t, :, :].unsqueeze(2).broadcast_to([P, 2, H2, SQ])
                        view = tanh_buf(s, t).rearrange("p (e h q) -> p e h q", e=2, h=H2)
                        tt(view, view, seen, ALU.mult).then_inc(sm["at_f"], 1)
                    for t in range(TT):
                        dve.wait_ge(sm["at_hi"], v.two[t])
                        lo_part(AT[s][:, 1, t, :], tanh_buf(s, t), AT[s][:, 0, t, :]).then_inc(sm["at_lo"], 1)
                elif k == 3:
                    for t in range(TT):
                        dve.wait_ge(sm["rs_hi"], v.two[t])
                        at = slice(t * 512, t * 512 + 512)
                        lo_part(RS[s][32:SQ, at], bank(s, t)[32:SQ, :], RS[s][32:SQ, at]).then_inc(sm["rs_lo"], 1)
                    for i in range(4):
                        t, c = i // 2, i % 2
                        dve.wait_ge(sm["ah_hi"], v.four[i])
                        at = slice(t * 512, t * 512 + 512)
                        lo_part(WIDE[s][:, 1, c, at], bank(s, 2 * (1 - t) + c), WIDE[s][:, 0, c, at]
                                ).then_inc(sm["ah_lo"], 1)
                elif k == 4:
                    for h in range(H2):
                        dve.wait_ge(sm["ct_hi"], v.four[h])
                        hi, lo = ((CT[s][:, 0, :], CT[s][:, 1, :]) if h % 2 == 0
                                  else (AT[s][:, 0, 0, :], AT[s][:, 1, 0, :]))
                        stt(lo, bank(s, h % 2), 0.0, hi.bitcast(F32), ALU.max, ALU.subtract
                            ).then_inc(sm["ct_lo"], 1)
                else:
                    dve.wait_ge(sm["hat_hi"], n)
                    lo_part(CT[s][:, 1, :], bank(s, 0), CT[s][:, 0, :]).then_inc(sm["hat_lo"], 1)
                    for t, b in enumerate((3, 1)):
                        dve.wait_ge(sm["gate_t"], v.two[t])
                        last = tt(F[s][:, 512 + t * D:512 + t * D + D], bank(s, b)[:, 0:D], F[s][:, t * D:t * D + D],
                                  ALU.subtract)
                    last.then_inc(sm["gate"], 1)
                    ts(XN[s][:, :], XN[s][:, :], 0.5, 0.5, ALU.mult, ALU.add).then_inc(sm["gate"], 1)
                    dve.wait_ge(sm["gate"], v.att[1])
                    tt(XN[s][:, :], XN[s][:, :], F[s][:, 512:1024], ALU.mult).then_inc(sm["gate"], 1)
                    dve.wait_ge(sm["x_ha"], n)
                    dve.wait_ge(sm["gate"], v.att[2])
                    tt(X[s][:, :], X[s][:, :], XN[s][:, :], ALU.add).then_inc(sm["res2"], 1)

            def step(s, what, v):
                kind, which, k = what
                if kind == "att":
                    att(s, which, k, v)
                else:
                    l2(s, k, v)

            passes(dve, step)


def kernel(**inputs):
    import concourse.bacc as bacc
    from concourse.bass_utils import run_bass_kernel_spmd

    a = {k: np.asarray(v) for k, v in inputs.items()}
    x, adj = a["x"], a["adj"]
    boards = x.shape[0]
    W = a["L2_gnn_W"]
    mats = ([a[f"L0_gnn_W{k}"].T for k in "qkvo"] + [a[f"L{n}_gnn_W{k}"] for n in (1, 3) for k in "qkvo"]
            + list(W) + [w.T for w in W] + [w.T for w in a["L2_gnn_attn"]]
            + list(a["L2_gnn_A_w"].T.reshape(H2, D, D))
            + [a["L2_gnn_fc_w"].T, a["L2_gnn_fc_w"], a["L2_gnn_g1_w"].T, a["L2_gnn_g2_w"].T])
    chunks = lambda b: b.reshape(-1, P).T
    cols = np.concatenate([chunks(a["L0_gnn_bq"]), chunks(a["L0_gnn_bk"]), chunks(a["L2_gnn_bW"])], axis=1)
    rows = np.zeros((SQ, H2 * D), np.float32)
    rows[[0, 1, 32]] = a["L2_gnn_bW"].reshape(-1)
    rows[2:4] = np.concatenate([a["L0_gnn_bv"], a["L0_gnn_bo"], a["L1_gnn_bo"], a["L3_gnn_bo"]])
    rows[4:6, 0:D] = a["L2_gnn_gbias"]
    arrays = {
        "x": x.reshape(-1, D),
        "adjq": adj.transpose(1, 0, 2),
        "adjt": adj.reshape(boards // 2, 2, SQ, SQ).transpose(1, 3, 0, 2),
        "mats": np.stack(mats), "cols": cols, "rows": rows, "board_consts": constants(),
    }
    nc = bacc.Bacc("TRN2", target_bir_lowering=False, num_devices=1)
    arrays = {k: np.ascontiguousarray(v) for k, v in arrays.items()}
    args = [nc.dram_tensor(k, v.shape, mybir.dt.from_np(v.dtype), kind="ExternalInput").ap() for k, v in arrays.items()]
    out = nc.dram_tensor("out", (boards * SQ, D), F32, kind="ExternalOutput").ap()
    build(nc, *args, out)
    r = run_bass_kernel_spmd(nc, [arrays], core_ids=[0])
    return r.results[0]["out"].reshape(boards, SQ, D)
```

```python
from contextlib import ExitStack

import concourse.bass as bass
import numpy as np
from concourse import mybir

F32 = mybir.dt.float32
F32R = mybir.dt.float32r
BF16 = mybir.dt.bfloat16
U8 = mybir.dt.uint8
ALU = mybir.AluOpType
ACT = mybir.ActivationFunctionType
AX_X = mybir.AxisListType.X

P = 128
SQ = 64
D = 256
DC = D // P
NB = 4
TOK = NB * SQ
TT = TOK // P
H2 = 4
L2 = 3
LO = 32
RH = LO + H2
SLOTS = 2
EPS = 1e-5
MASKED = -1e30

ATT = [dict(layer=0, heads=8, mats=0, bias=1), dict(layer=1, heads=4, mats=4, bias=2),
       dict(layer=3, heads=4, mats=8, bias=3)]
M_G, M_W, M_A, M_FG, M_G2, MATS = 12, 16, 20, 24, 26, 27
R_WNAT, R_WT, R_ATT, R_AW, R_FCT, R_FCNAT, R_G1T, R_G2T, RAW = 12, 16, 20, 24, 28, 29, 30, 31, 32
C_ID, C_EYE, C_STATIC, C_ONES, C_SEL1, C_SEL2, C_RT, C_SELAB, C_HALF, C_HEADS, CST = (
    0, 128, 192, 384, 512, 640, 768, 896, 898, 899, 903)

SPLITS = [(M_W, R_WT, 4), (0, 0, 4), (4, 4, 4), (8, 8, 4), (M_A, R_AW, 4), (M_FG, R_FCT, 1), (M_G2, R_G2T, 1)]


def constants():
    c = np.zeros((P, CST), np.float32)
    c[:, C_ID:C_ID + P] = np.eye(P)
    sq = np.arange(SQ)
    r, f = sq // 8, sq % 8
    dr, df = abs(r[:, None] - r[None]), abs(f[:, None] - f[None])
    eye = np.eye(SQ, dtype=bool)
    masks = [f[:, None] == f[None], r[:, None] == r[None],
             r[:, None] - f[:, None] == r[None] - f[None], r[:, None] + f[:, None] == r[None] + f[None],
             (dr == 2) & (df == 1) | (dr == 1) & (df == 2) | eye, (dr <= 1) & (df <= 1)]
    for half in range(2):
        rows = slice(SQ * half, SQ * half + SQ)
        c[rows, C_EYE:C_EYE + SQ] = np.where(eye, 0, MASKED)
        for pair in range(3):
            at = C_STATIC + SQ * pair
            c[rows, at:at + SQ] = np.where(masks[2 * pair + half], 0, MASKED)
    c[:, C_ONES + np.array([0, 1, 32])] = 1
    c[0:4, C_SEL1:C_SEL1 + P] = 0
    c[2:4, C_SEL1:C_SEL1 + P] = 1
    c[4:6, C_SEL2:C_SEL2 + P] = 1
    c[[0, 2, 4, 32], C_SELAB] = 1
    c[[1, 3, 5], C_SELAB + 1] = 1
    for part in (0, LO):
        rows = np.arange(part, part + H2)
        c[rows, C_HEADS + rows - part] = 1
        c[rows, C_RT:C_RT + P] = 1
    c[:, C_HALF] = -0.5
    return c


H_BANKS, O_BANKS, Y_BANKS = (0, 3), (2, 0), (2, 3)
E_BANKS, HEAD_BANKS, G_BANKS, HAT_BANKS = (2, 3, 0, 1), (3, 1), (0, 1), (3, 2)

ORDER = {
    "pe": (44, (
        0, 0, 0, 0, 0, 0, 2, 0, 0, 1, 0, 0, 0, 3, 0, 0, 0, 0, 2, 1, 0, 0, 0, 0, 1, 2, 0, 1, 0, 2, 0, 0, 1,
        0, 2, 2, 0, 1, 4, 0, 0, 2, 0, 0, 2, 0, 0, 0, 3, 0, 0, 0, 1, 1, 2, 2, 0, 4, 3, 0, 1, 0, 1, 0, 0, 0,
        4, 0, 1, 2, 0, 0, 11, 1, 2, 2, 0, 0, 2, 2, 4, 0, 0, 0, 0, 2, 0, 1, 0, 1, 1, 3, 0, 1, 1, 1, 0, 0, 0,
        0, 0, 0, 0, 1, 12, 0, 0, 1, 0, 0, 8)),
    "act": (44, (
        0, 0, 0, 0, 0, 0, 2, 1, 0, 0, 1, 0, 0, 2, 0, 1, 0, 0, 1, 1, 0, 0, 0, 0, 0, 1, 0, 2, 0, 0, 0, 0, 1,
        0, 0, 7, 0, 0, 0, 0, 1, 5, 0, 1, 0, 1, 0, 1, 1, 3, 0, 0, 0, 2, 2, 0, 1, 3, 3, 0, 1, 0, 0, 4, 0, 0,
        2, 0, 0, 2, 3, 0, 5, 1, 6, 0, 2, 1, 2, 1, 0, 0, 0, 0, 0, 2, 0, 0, 1, 1, 6, 5, 0, 0, 2, 5, 0, 0, 0,
        0, 1, 2, 0, 1, 1, 0, 2, 0, 3, 2, 3)),
    "dve": (49, (
        1, 0, 1, 2, 0, 0, 3, 0, 1, 1, 0, 0, 0, 2, 0, 0, 1, 0, 0, 0, 0, 0, 0, 1, 0, 0, 0, 3, 0, 1, 1, 0, 1,
        0, 4, 1, 0, 3, 2, 0, 0, 3, 0, 1, 0, 4, 0, 1, 0, 1, 1, 0, 2, 1, 2, 0, 0, 2, 2, 0, 1, 2, 0, 1, 0, 0,
        3, 0, 0, 0, 3, 0, 11, 2, 2, 1, 0, 3, 2, 5, 0, 0, 0, 0, 0, 2, 0, 0, 0, 1, 3, 1, 0, 3, 1, 2, 1, 0, 0,
        0, 0, 3, 0, 1, 3, 0, 1, 0, 1, 0, 3)),
    "pool": (41, (
        0, 1, 0, 0, 0, 0, 1, 0, 2, 1, 0, 0, 0, 1, 0, 0, 1, 0, 0, 1, 0, 0, 0, 2, 0, 0, 0, 0, 0, 3, 0, 0, 6,
        0, 11, 0, 0, 0, 0, 0, 0, 4, 0, 0, 0, 0, 0, 0, 2, 0, 0, 0, 0, 2, 1, 0, 1, 0, 7, 0, 2, 2, 0, 2, 0, 0,
        3, 1, 0, 1, 2, 0, 1, 1, 5, 1, 4, 3, 1, 1, 0, 0, 2, 0, 0, 2, 0, 0, 2, 2, 5, 6, 1, 3, 1, 3, 2, 1, 0,
        0, 0, 0, 1, 0, 1, 0, 0, 1, 0, 0, 1)),
}


class Counts:

    def __init__(self, i, keep=lambda x: x, later=False):
        self.once = keep(i + 1)
        self.before = keep(i * 16) if later else None
        self.two = [keep(i * 2 + (n + 1)) for n in range(2)]
        self.four = [keep(i * 4 + (n + 1)) for n in range(4)]
        self.six = [keep(i * 6 + (n + 1)) for n in range(6)]
        self.eight = [keep(i * 8 + (n + 1)) for n in range(8)]
        self.att = [keep(i * 3 + (n + 1)) for n in range(3)]
        self.dma = keep(i * 16 + 16)
        self.dma2 = keep(i * 32 + 32)


def build(nc, x_in, adjq_in, adjt_in, mats_in, cols_in, rows_in, cst_in, out):
    GROUPS = x_in.shape[0] // TOK
    ITERS = GROUPS // SLOTS
    x_v = x_in.rearrange("(g t p) d -> p g t d", t=TT, p=P)
    out_v = out.rearrange("(g t p) d -> p g t d", t=TT, p=P)
    adjq_v = adjq_in.rearrange("q (g b) k -> q g (b k)", b=NB)
    adjt_v = adjt_in.rearrange("e k (g t) q -> e k g t q", t=TT)

    ctx = ExitStack()
    with ctx:
        def sb(name, shape, dt, scope=ctx):
            return scope.enter_context(nc.sbuf_tensor(name, shape, dt))

        def sem(name):
            return ctx.enter_context(nc.semaphore(name))

        WHI = sb("w_hi", [P, MATS, DC, D], F32R)
        WLO = sb("w_lo", [P, MATS, DC, D], F32R)
        ROWS = sb("bias_rows", [SQ, H2 * D], F32R)
        SELR = sb("sel_rows", [P, 4, P], F32R)
        CF = sb("consts", [P, P + SQ + 1 + H2], F32)
        STATIC = sb("static_masks", [P, 3, SQ], BF16)
        COLS = sb("bias_cols", [P, 12], F32)
        CVEC = sb("c_vec", [P, DC, H2], F32)
        UVEC = sb("u_vec", [P, 2, DC, RH], F32R)
        S0 = sb("s0", [RH, 1], F32)
        IDENT = CF[:, 0:P]
        EYE = CF[:, P:P + SQ]
        HALF = CF[:, P + SQ:P + SQ + 1]
        HEADS = CF[0:RH, P + SQ + 1:P + SQ + 1 + H2]

        X, XN, HT, MASKA, MASKO, ADJ8, ADJT8, SMALL = ([] for _ in range(8))
        for s in range(SLOTS):
            X.append(sb(f"x{s}", [P, TT * D], F32))
            XN.append(sb(f"xn{s}", [P, TT * D], F32))
            HT.append(sb(f"hT{s}", [P, 2, DC, TOK], F32R))
            MASKA.append(sb(f"mask_adj{s}", [P, TOK], BF16))
            MASKO.append(sb(f"mask_adj_eye{s}", [P, TOK], BF16))
            ADJ8.append(sb(f"adj8_{s}", [P, TOK], U8))
            ADJT8.append(sb(f"adjT8_{s}", [P, TT, 2, SQ], U8))
            SMALL.append(sb(f"small{s}", [P, 68], F32))
        STATS = [m[:, 0:12].rearrange("p (t c) -> p t c", t=TT) for m in SMALL]
        MV = [m[:, 12:16].rearrange("p (t c) -> p t c", t=TT) for m in SMALL]
        VE = [m[:, 16:18] for m in SMALL]
        RSTD = [m[:, 18:20] for m in SMALL]
        ROWMAX = [m[:, 20:36] for m in SMALL]
        ROWSUM = [m[:, 36:52] for m in SMALL]
        RECIP = [m[:, 52:68] for m in SMALL]

        scope = ExitStack()
        RAWM = sb("raw_mats", [P, RAW, DC, D], F32, scope)
        T1 = RAWM[:, R_WT:R_WT + H2, :, :]
        RAWR = sb("raw_rows", [SQ, H2 * D], F32, scope)
        RAWRH = HT[0][0:SQ, :, :, :].rearrange("p j c k -> p (j c k)")
        RAWC = sb("raw_consts", [P, CST], F32, scope)
        A1 = sb("attn_b", [P, DC, H2], F32, scope)
        S0M = sb("s0_matrix", [RH, H2], F32, scope)
        BPAD = sb("b_padded", [P, DC, RH], F32, scope)
        UPAD = sb("u_padded", [P, DC, RH], F32, scope)
        scope.close()
        scope = ExitStack()
        Q, K, V, PR, PTS, OT, R4 = ([] for _ in range(7))
        for s in range(SLOTS):
            Q.append(sb(f"qT{s}", [P, DC, TOK], F32, scope))
            K.append(sb(f"kT{s}", [P, DC, TOK], F32, scope))
            V.append(sb(f"v{s}", [P, TT, D], F32, scope))
            PR.append(sb(f"probs{s}", [P, 2, 512], F32, scope))
            PTS.append(sb(f"probsT{s}", [P, 2, 512], F32, scope))
            OT.append(sb(f"oT{s}", [P, 2, DC, TOK], F32R, scope))
            sb(f"pad_a{s}", [P, 1536], F32, scope)
            R4.append(sb(f"row_terms{s}", [P, 1024], F32R, scope))
            sb(f"pad_b{s}", [P, 2048], F32, scope)
        scope.close()
        scope = ExitStack()
        WIDE, AT, F, RS, CT = ([] for _ in range(5))
        for s in range(SLOTS):
            WIDE.append(sb(f"wide{s}", [P, 2, DC, TOK * H2], F32R, scope))
            AT.append(sb(f"aT{s}", [P, 2, TT, 512], F32R, scope))
            F.append(sb(f"f{s}", [P, 1024], F32, scope))
            RS.append(sb(f"rs{s}", [SQ, TOK * H2], F32R, scope))
            CT.append(sb(f"cT{s}", [P, 2, 512], F32R, scope))
        scope.close()

        PS = ctx.enter_context(nc.psum_tensor("ps", [P, 8, 512], F32))

        def bank(s, n):
            return PS[:, 4 * s + n, :]

        def o_view(s, c):
            return PS[:, 4 * s + O_BANKS[c]:4 * s + O_BANKS[c] + 2, 0:P].rearrange("p e (t q) -> p t e q", q=SQ)

        def e_view(s, part, oc, h):
            return WIDE[s][:, part, oc, :].rearrange("p (b h q) -> p b h q", h=H2, q=SQ)[:, :, h, :]

        def e_bank(s, b, oc):
            return bank(s, b)[:, oc * TOK:oc * TOK + TOK].rearrange("p (b q) -> p b q", q=SQ)

        def tanh_buf(s, t):
            return XN[s][:, :] if t == 0 else F[s][:, 0:512]

        ONCE = ["r_ps", "r_hi", "r_lo", "r4_ready", "hh_ready", "hl_ready", "ha_sb", "x_ha", "res2"]
        TWICE = ["s2_ps", "tanh", "at_f", "at_hi", "at_lo", "rs_ps", "rs_hi", "rs_lo", "hat_ps", "hat_hi", "hat_lo",
                 "g_ps", "gate_t", "diff", "gated", "masks"]
        FOUR = ["e_ps", "e_hi", "e_lo", "ah_ps", "ah_hi", "ah_lo", "hp_ps", "ct_hi", "ct_lo", "ha_mm"]
        NORM = ["bn", "var", "ve", "rstd", "xn_ready", "hT_ps", "hT_hi", "hT_lo"]
        ATTS = ["q_ps", "k_ps", "v_ps", "q_sb", "k_sb", "v_sb", "s_ps", "masked", "rowmax", "exp", "recip", "probs",
                 "pt_ps", "pt_sb", "o_ps", "oT_hi", "oT_lo", "y_ps", "res"]
        S = [{n: sem(f"{n}_{s}") for n in ONCE + TWICE + FOUR + NORM + ATTS + ["x_in", "adj_in", "adjT_in", "stored"]}
             for s in range(SLOTS)]
        raw_sems = [sem(f"raw_in{n}") for n in range(2, RAW // 4)]
        cst_ready, setup = sem("consts_in"), {n: sem(n) for n in (
            "consts", "waited", "rows", "w_hi", "w_lo", "t1_ps", "t1_sb", "g_ps", "g_hi", "g_lo",
            "vec_ps", "vec_sb", "u", "zeroed")}

        block = ctx.enter_context(nc.Block())

        NORM_OF = (0, 1, 3, 2)

        def norm_count(a, v):
            return v.four[NORM_OF[a]]

        def units(a):
            first, blocks = ((0, 2), (4, 1), (6, 1))[a]
            return [(first + 2 * j + cj, 2 * j + cj, j, cj) for j in range(blocks) for cj in range(2)]

        def turned(a):
            us = units(a)
            return [us[0:2], us[2:4]] if len(us) == 4 else [us[0:1], us[1:2]]

        def norm_halves(a, v):
            return v.eight[2 * NORM_OF[a]:2 * NORM_OF[a] + 2]

        def att_steps(a):
            us = units(a)
            softmax = []
            for i in range(len(us) + 1):
                softmax += [("mask", a, u) for u in us[i:i + 1]] + [("max", a, u) for u in us[max(i - 1, 0):i]]
            return ([("bn", a, 0), ("bn", a, 1), ("stats", a, 0), ("norm", a, 0)] + [("masks", a, 0)] * (a == 0)
                    + [("turn", a, 0), ("turn", a, 1), ("q", a, 0), ("k", a, 0), ("v", a, 0)]
                    + [("scores", a, u) for u in us] + softmax + [("soft", a, u) for u in us]
                    + [("pt", a, 0), ("pt", a, 1), ("pv", a, 0), ("pv", a, 1), ("out", a, 0), ("out", a, 1)])

        L2_STEPS = ([("bn", L2, 0), ("bn", L2, 1), ("stats", L2, 0), ("norm", L2, 0), ("turn", L2, 0), ("turn", L2, 1),
                     ("r", L2, 0)] + [("e", L2, h) for h in range(H2)]
                    + [("h", L2, 0), ("s2", L2, 0), ("s2", L2, 1), ("a", L2, 0), ("a", L2, 1), ("ah", L2, 0), ("ah", L2, 1),
                       ("hp", L2, 0), ("hp", L2, 1), ("ha", L2, 0), ("hp", L2, 2), ("ha", L2, 1), ("hp", L2, 3),
                       ("hf", L2, 0), ("ha", L2, 2), ("ha", L2, 3), ("hf", L2, 1), ("hat", L2, 0), ("hat", L2, 1),
                       ("g", L2, 0), ("g", L2, 1), ("sum", L2, 0)])
        STEPS = att_steps(0) + att_steps(1) + L2_STEPS + att_steps(2)

        def passes(eng, step, order):
            n = len(STEPS)
            lag, merge = order
            assert len(merge) == n and sum(merge) == n

            def turn(first, now, before):
                done = 0
                for k in range(n):
                    step(0, STEPS[k], now)
                    for done in range(done + 1, done + merge[k] + 1):
                        if done > lag:
                            step(1, STEPS[done - lag - 1], now)
                        elif not first:
                            step(1, STEPS[n - lag + done - 1], before)

            turn(True, Counts(0), None)
            if ITERS > 1:
                with eng.Fori(0, ITERS - 1) as i:
                    turn(False, Counts(i + 1, eng.snap, later=True), Counts(i, eng.snap))
            last = Counts(ITERS - 1)
            for k in range(n - lag, n):
                step(1, STEPS[k], last)

        def alone(eng):
            eng.sem_inc(setup["waited"], 1)

        @block.sync
        def _(sp):
            sp.dma_start(RAWC[:, :], cst_in).then_inc(cst_ready, 16)
            sp.dma_start(COLS[:, :], cols_in).then_inc(cst_ready, 16)
            sp.dma_start(RAWR[:, :], rows_in).then_inc(cst_ready, 16)
            for n in (4, 3, 5, 0, 1, 2, 6, 7):
                sp.dma_start(RAWM[:, 4 * n:4 * n + 4, :, :],
                             mats_in[4 * n:4 * n + 4, :, :].rearrange("m (c p) o -> p m c o", p=P)
                             ).then_inc(raw_sems[max(n - 2, 0)], 16)
            sp.wait_ge(setup["zeroed"], 1)

            def load_x(s, g):
                sp.dma_start(X[s][:, :].rearrange("p (t d) -> p t d", t=TT), x_v[:, g, :, :]).then_inc(S[s]["x_in"], 16)

            def load_adj(s, g):
                for half in range(2):
                    sp.dma_start(ADJ8[s][SQ * half:SQ * half + SQ, :], adjq_v[:, g, :]).then_inc(S[s]["adj_in"], 16)

            def load_adjT(s, g):
                for e in range(2):
                    sp.dma_start(ADJT8[s][SQ * e:SQ * e + SQ, :, e, :], adjt_v[e, :, g, :, :]
                                 ).then_inc(S[s]["adjT_in"], 16)

            for s in range(SLOTS):
                load_x(s, s)
                load_adj(s, s)
                load_adjT(s, s)

            def turn(s, g, gnext, now):
                if gnext is not None:
                    sp.wait_ge(S[s]["masks"], now.two[0])
                    alone(sp)
                    sp.wait_ge(S[s]["at_f"], now.two[1])
                    alone(sp)
                    load_adj(s, gnext)
                    load_adjT(s, gnext)
                sp.wait_ge(S[s]["res"], now.six[5])
                if gnext is not None:
                    alone(sp)
                    load_x(s, gnext)
                sp.dma_start(out_v[:, g, :, :], XN[s][:, :].rearrange("p (t d) -> p t d", t=TT)
                             ).then_inc(S[s]["stored"], 16)

            if ITERS > 1:
                with sp.Fori(0, ITERS - 1) as i:
                    now = Counts(i, sp.snap)
                    for s in range(SLOTS):
                        turn(s, sp.snap(i * SLOTS + s), sp.snap(i * SLOTS + SLOTS + s), now)
            for s in range(SLOTS):
                turn(s, GROUPS - SLOTS + s, None, Counts(ITERS - 1))
                sp.wait_ge(S[s]["stored"], 16 * ITERS)

        @block.gpsimd
        def _(pool):
            nc.gpsimd.memset(UPAD[:, :, :], 0.0)
            nc.gpsimd.memset(BPAD[:, :, :], 0.0)
            for s in range(SLOTS):
                last = nc.gpsimd.memset(ADJT8[s][:, :, :, :], 0.0)
            last.then_inc(setup["zeroed"], 1)

            def step(s, what, v):
                k, a, i = what
                sm = S[s]
                if k == "stats":
                    n = norm_count(a, v)
                    pool.wait_ge(sm["ve"], n)
                    nc.gpsimd.tensor_tensor(RSTD[s], VE[s], HALF.broadcast_to([P, TT]), ALU.pow
                                            ).then_inc(sm["rstd"], 1)
                elif k == "r":
                    pool.wait_ge(sm["r_lo"], v.once)
                    nc.gpsimd.tensor_tensor(
                        R4[s][0:RH, :].rearrange("p (b h q) -> p b h q", h=H2, q=SQ),
                        RS[s][0:RH, 0:TOK].bitcast(F32).rearrange("p (b q) -> p b q", q=SQ).unsqueeze(2).broadcast_to([RH, NB, H2, SQ]),
                        HEADS.unsqueeze(1).unsqueeze(3).broadcast_to([RH, NB, H2, SQ]), ALU.mult
                        ).then_inc(sm["r4_ready"], 1)
                elif k == "hat" and i == 0:
                    pool.wait_ge(sm["ha_sb"], v.once)
                    nc.gpsimd.tensor_tensor(X[s][:, :], X[s][:, :], F[s][:, 0:512], ALU.add).then_inc(sm["x_ha"], 1)

            pool.wait_ge(setup["consts"], 1)
            passes(pool, step, ORDER["pool"])

        @block.tensor
        def _(pe):
            def mm(o, lhsT, rhs, start, stop):
                return nc.tensor.matmul(o, lhsT, rhs, start=start, stop=stop, skip_group_check=True)

            def split3(o, terms, start=True, stop=True):
                n = 3 * len(terms)
                i = 0
                for lh, ll, rh, rl in terms:
                    for a, b in ((lh, rh), (lh, rl), (ll, rh)):
                        last = mm(o, a, b, start and i == 0, stop and i == n - 1)
                        i += 1
                return last

            bcol = COLS[:, 4:12].rearrange("p (h c) -> p h c", h=H2)
            pe.wait_ge(setup["consts"], 1)
            pe.wait_ge(raw_sems[1], 16)
            pe.wait_ge(raw_sems[3], 16)
            for h in range(H2):
                for oc in range(DC):
                    for c in range(DC):
                        last = mm(PS[:, h, oc * D:oc * D + D], RAWM[:, R_ATT + h, c, oc * P:oc * P + P],
                                  RAWM[:, R_WNAT + h, c, :], c == 0, c == DC - 1)
                last.then_inc(setup["t1_ps"], 1)
            for h in range(H2):
                for oc in range(DC):
                    for c in range(DC):
                        last = mm(PS[:, 4, oc * H2 + h:oc * H2 + h + 1], RAWM[:, R_ATT + h, c, oc * P:oc * P + P],
                                  bcol[:, h, c:c + 1], c == 0, c == DC - 1)
            last.then_inc(setup["vec_ps"], 1)
            for h in range(H2):
                pe.wait_ge(setup["t1_sb"], h + 1)
                for ic in range(DC):
                    for c in range(DC):
                        last = mm(PS[:, h, ic * D:ic * D + D], RAWM[:, R_WNAT + h, c, ic * P:ic * P + P],
                                  T1[:, h, c, :], c == 0, c == DC - 1)
                last.then_inc(setup["g_ps"], 1)
            pe.wait_ge(raw_sems[5], 16)
            for ic in range(DC):
                for c in range(DC):
                    last = mm(PS[:, 5, ic * D:ic * D + D], RAWM[:, R_FCNAT, c, ic * P:ic * P + P],
                              RAWM[:, R_G1T, c, :], c == 0, c == DC - 1)
            last.then_inc(setup["g_ps"], 1)
            pe.wait_ge(setup["vec_sb"], 1)
            for h in range(H2):
                for ic in range(DC):
                    for c in range(DC):
                        at = ic * H2 + h
                        mm(PS[:, 6, at:at + 1], T1[:, h, c, ic * P:ic * P + P], bcol[:, h, c:c + 1],
                           c == 0, c == DC - 1)
                        mm(PS[:, 7, at:at + 1], RAWM[:, R_WNAT + h, c, ic * P:ic * P + P], A1[:, c, h:h + 1],
                           c == 0, c == DC - 1)
            for c in range(DC):
                last = mm(PS[0:RH, 4, 0:H2], BPAD[:, c, :], A1[:, c, :], c == 0, c == DC - 1)
            last.then_inc(setup["vec_ps"], 1)
            pe.wait_ge(setup["consts"], 2)
            pe.wait_ge(setup["zeroed"], 1)
            pe.wait_ge(setup["w_lo"], len(SPLITS))
            pe.wait_ge(setup["g_lo"], H2 + 1)
            pe.wait_ge(setup["vec_sb"], 3)
            pe.wait_ge(setup["rows"], 4)

            def transposed_h(s, a, c, v):
                for t in range(TT):
                    if c == 0:
                        pe.wait_ge(S[s]["xn_ready"], norm_halves(a, v)[t])
                    last = nc.tensor.transpose(bank(s, H_BANKS[c])[:, t * P:t * P + P],
                                               XN[s][:, t * D + c * P:t * D + c * P + P], IDENT)
                last.then_inc(S[s]["hT_ps"], 1)

            def features_out(s, o, m, oc, halves=None):
                for c in range(DC):
                    if halves:
                        pe.wait_ge(S[s]["hT_hi"], halves[c])
                    mm(o, WHI[:, m, c, oc * P:oc * P + P], HT[s][:, 0, c, :], c == 0, False)
                    mm(o, WLO[:, m, c, oc * P:oc * P + P], HT[s][:, 0, c, :], False, False)
                for c in range(DC):
                    if halves:
                        pe.wait_ge(S[s]["hT_lo"], halves[c])
                    last = mm(o, WHI[:, m, c, oc * P:oc * P + P], HT[s][:, 1, c, :], False, c == DC - 1)
                return last

            def tokens_out(o, actT, t, m, bias=None, start=True, ready=(), halves=()):
                at = slice(t * P, t * P + P)
                for c in range(DC):
                    if ready and t == 0:
                        pe.wait_ge(ready[0], halves[c])
                    mm(o, actT(0, c)[:, at], WHI[:, m, c, :], start and c == 0, False)
                    mm(o, actT(0, c)[:, at], WLO[:, m, c, :], False, False)
                for c in range(DC):
                    if ready and t == 0:
                        pe.wait_ge(ready[1], halves[c])
                    last = mm(o, actT(1, c)[:, at], WHI[:, m, c, :], False, bias is None and c == DC - 1)
                if bias is not None:
                    last = mm(o, SELR[0:SQ, 1, :], ROWS[:, bias * D:bias * D + D], False, True)
                return last

            def att(s, k, a, i, v):
                sm, L, n = S[s], ATT[a], v.att[a]
                hd = D // L["heads"]
                two = L["heads"] == 8
                if k == "turn":
                    transposed_h(s, a, i, v)
                elif k in ("q", "k"):
                    b = 1 if k == "q" else 2
                    for oc in range(DC):
                        last = features_out(s, bank(s, b)[:, oc * TOK:oc * TOK + TOK], L["mats"] + b - 1, oc,
                                            norm_halves(a, v) if k == "q" and oc == 0 else None)
                    last.then_inc(sm[k + "_ps"], 1)
                elif k == "v":
                    for t in range(TT):
                        last = tokens_out(bank(s, 3)[:, t * D:t * D + D], lambda j, c: HT[s][:, j, c, :], t,
                                          L["mats"] + 2, 0 if a == 0 else None)
                    last.then_inc(sm["v_ps"], 1)
                elif k == "scores":
                    _, m, j, cj = i
                    if m == 0:
                        pe.wait_ge(sm["q_sb"], n)
                        pe.wait_ge(sm["k_sb"], n)
                        alone(pe)
                    if m == 3:
                        pe.wait_ge(sm["v_sb"], n)
                        alone(pe)
                    for b in range(NB):
                        for half in range(2):
                            h = 2 * (j + (2 if two else 1) * cj) + half
                            r, c = h * hd % P, h * hd // P
                            last = mm(bank(s, m)[SQ * half:SQ * half + SQ, b * SQ:b * SQ + SQ],
                                      Q[s][r:r + hd, c, b * SQ:b * SQ + SQ],
                                      K[s][r:r + hd, c, b * SQ:b * SQ + SQ], True, True)
                    last.then_inc(sm["s_ps"], 1)
                elif k == "pt":
                    for u, _, j, cj in turned(a)[i]:
                        pe.wait_ge(sm["probs"], v.eight[u])
                        for at in range(cj * TOK, cj * TOK + TOK, P):
                            last = nc.tensor.transpose(bank(s, 1 - i)[:, at:at + P], PR[s][:, j, at:at + P], IDENT)
                    last.then_inc(sm["pt_ps"], 1)
                elif k == "pv":
                    if i == 0:
                        pe.wait_ge(sm["v_sb"], n)
                    pe.wait_ge(sm["pt_sb"], v.six[2 * a + (1 if two else i)])
                    alone(pe)
                    for h in range(i * L["heads"] // 2, (i + 1) * L["heads"] // 2):
                        r, half, blocks = h * hd % P, h % 2, 2 if two else 1
                        j, cj = h // 2 % blocks, h // 2 // blocks
                        for t in range(TT):
                            for e in range(2):
                                at = cj * 256 + t * P + half * SQ
                                last = mm(bank(s, O_BANKS[i] + e)[r:r + hd, t * SQ:t * SQ + SQ],
                                          V[s][SQ * e:SQ * e + SQ, t, h * hd:h * hd + hd],
                                          PTS[s][SQ * e:SQ * e + SQ, j, at:at + SQ], True, True)
                    last.then_inc(sm["o_ps"], 1)
                elif k == "out":
                    if i == 0:
                        pe.wait_ge(sm["oT_lo"], v.six[2 * a])
                    tokens_out(bank(s, Y_BANKS[i])[:, 0:D], lambda j, c: OT[s][:, j, c, :], i, L["mats"] + 3,
                               L["bias"], ready=(sm["oT_hi"], sm["oT_lo"]), halves=v.six[2 * a:]).then_inc(sm["y_ps"], 1)

            def l2(s, k, i, v):
                sm, n = S[s], v.once
                wide = lambda j, c: WIDE[s][:, j, c, :]
                ct = lambda h: (CT[s][:, 0, :], CT[s][:, 1, :]) if h % 2 == 0 else (AT[s][:, 0, 0, :], AT[s][:, 1, 0, :])
                if k == "turn":
                    transposed_h(s, L2, i, v)
                elif k == "r":
                    o = bank(s, 1)[0:RH, 0:TOK]
                    for c in range(DC):
                        pe.wait_ge(sm["hT_hi"], norm_halves(L2, v)[c])
                        mm(o, UVEC[:, 0, c, :], HT[s][:, 0, c, :], c == 0, False)
                        mm(o, UVEC[:, 1, c, :], HT[s][:, 0, c, :], False, False)
                    for c in range(DC):
                        pe.wait_ge(sm["hT_lo"], norm_halves(L2, v)[c])
                        last = mm(o, UVEC[:, 0, c, :], HT[s][:, 1, c, :], False, c == DC - 1)
                    last.then_inc(sm["r_ps"], 1)
                elif k == "e":
                    if i == H2 - 1:
                        pe.wait_ge(sm["r_lo"], n)
                    for oc in range(DC):
                        last = features_out(s, bank(s, E_BANKS[i])[:, oc * TOK:oc * TOK + TOK], M_G + i, oc)
                    last.then_inc(sm["e_ps"], 1)
                elif k == "s2":
                    o = bank(s, 2 + i)
                    keys = lambda j, c: HT[s][:, j, c, i * P:i * P + P]
                    cols = slice(i * 512, i * 512 + 512)
                    if i == 0:
                        pe.wait_ge(sm["e_lo"], v.eight[1])
                        pe.wait_ge(sm["e_hi"], v.four[3])
                    for c in range(DC):
                        mm(o, keys(0, c), wide(0, c)[:, cols], c == 0, False)
                        mm(o, keys(1, c), wide(0, c)[:, cols], False, False)
                    for c in range(DC):
                        if i == 0:
                            pe.wait_ge(sm["e_lo"], v.eight[6 + c])
                        mm(o, keys(0, c), wide(1, c)[:, cols], False, False)
                    if i == 0:
                        pe.wait_ge(sm["r4_ready"], n)
                    mm(o, SELR[0:RH, 3, :], R4[s][0:RH, i * 512:i * 512 + 512], False, True
                       ).then_inc(sm["s2_ps"], 1)
                elif k == "a":
                    for j, part in enumerate(("at_hi", "at_lo")):
                        pe.wait_ge(sm[part], v.two[i])
                        last = mm(bank(s, i), SELR[:, 0, :], AT[s][:, j, i, :], j == 0, j == 1)
                    last.then_inc(sm["rs_ps"], 1)
                elif k == "ah":
                    for c in range(DC):
                        if i:
                            pe.wait_ge(sm["rs_lo"], v.two[c])
                        at = i * D + c * P
                        split3(bank(s, 2 * (1 - i) + c), [(CT[s][:, 0, at:at + P], CT[s][:, 1, at:at + P],
                                                           AT[s][:, 0, i, :], AT[s][:, 1, i, :])]
                               ).then_inc(sm["ah_ps"], 1)
                elif k == "hp":
                    part = lambda x: x.rearrange("p (b h q) -> p b h q", h=H2, q=SQ)[:, :, i, :]
                    if i == 0:
                        pe.wait_ge(sm["ah_lo"], v.four[1])
                    for oc in range(DC):
                        o = bank(s, HEAD_BANKS[i % 2])[:, oc * TOK:oc * TOK + TOK]
                        for c in range(DC):
                            if i == 0 and oc == 0:
                                pe.wait_ge(sm["ah_hi"], v.four[2 + c])
                            mm(o, WHI[:, M_W + i, c, oc * P:oc * P + P], part(wide(0, c)), c == 0, False)
                            mm(o, WLO[:, M_W + i, c, oc * P:oc * P + P], part(wide(0, c)), False, False)
                        mm(o, ROWS[:, i * D + oc * P:i * D + oc * P + P], part(RS[s][:, :]), False, False)
                        for c in range(DC):
                            if i == 0 and oc == 0:
                                pe.wait_ge(sm["ah_lo"], v.four[2 + c])
                            last = mm(o, WHI[:, M_W + i, c, oc * P:oc * P + P], part(wide(1, c)), False, c == DC - 1)
                    last.then_inc(sm["hp_ps"], 1)
                elif k == "ha":
                    hi, lo = ct(i)
                    tiles = [(t, c, c * TOK + t * P) for t in range(TT) for c in range(DC)]
                    pe.wait_ge(sm["ct_hi"], v.four[i])
                    for t, c, at in tiles:
                        mm(bank(s, 2)[:, t * D:t * D + D], hi[:, at:at + P], WHI[:, M_A + i, c, :],
                           i == 0 and t == 0 and c == 0, False)
                        mm(bank(s, 2)[:, t * D:t * D + D], hi[:, at:at + P], WLO[:, M_A + i, c, :], False, False)
                    pe.wait_ge(sm["ct_lo"], v.four[i])
                    for t, c, at in tiles:
                        last = mm(bank(s, 2)[:, t * D:t * D + D], lo[:, at:at + P], WHI[:, M_A + i, c, :],
                                  False, i == H2 - 1 and t == TT - 1 and c == DC - 1)
                    last.then_inc(sm["ha_mm"], 1)
                elif k == "hf":
                    o = bank(s, G_BANKS[i])
                    split3(o, [(HT[s][:, 0, c, i * P:i * P + P], HT[s][:, 1, c, i * P:i * P + P],
                                WHI[:, M_FG:M_FG + 2, c, :], WLO[:, M_FG:M_FG + 2, c, :]) for c in range(DC)],
                           stop=False)
                    mm(o[:, D:2 * D], SELR[0:SQ, 2, :], ROWS[:, 0:D], False, False)
                elif k == "hat":
                    if i == 0:
                        pe.wait_ge(sm["ha_sb"], n)
                    for t in range(TT):
                        last = nc.tensor.transpose(bank(s, HAT_BANKS[i])[:, t * P:t * P + P],
                                                   F[s][:, t * D + i * P:t * D + i * P + P], IDENT)
                    last.then_inc(sm["hat_ps"], 1)
                elif k == "g":
                    tokens_out(bank(s, G_BANKS[i])[:, D:2 * D], lambda j, c: CT[s][:, j, c * TOK:c * TOK + TOK], i,
                               M_G2, start=False, ready=(sm["hat_hi"], sm["hat_lo"]), halves=v.two).then_inc(sm["g_ps"], 1)

            def step(s, what, v):
                k, a, i = what
                if a == L2:
                    l2(s, k, i, v)
                else:
                    att(s, k, a, i, v)

            passes(pe, step, ORDER["pe"])

        @block.scalar
        def _(act):
            fn = nc.scalar.activation
            act.wait_ge(cst_ready, 48)
            fn(CF[:, 0:P + SQ], RAWC[:, C_ID:C_ID + P + SQ], ACT.Copy)
            fn(CF[:, P + SQ:P + SQ + 1 + H2], RAWC[:, C_HALF:C_HALF + 1 + H2], ACT.Copy).then_inc(setup["consts"], 1)
            fn(STATIC[:, :, :], RAWC[:, C_STATIC:C_STATIC + 3 * SQ], ACT.Copy)
            fn(SELR[:, :, :], RAWC[:, C_ONES:C_ONES + 4 * P], ACT.Copy).then_inc(setup["consts"], 1)
            fn(RAWRH[:, :], RAWR[:, :], ACT.Copy).then_inc(setup["rows"], 1)
            def split_hi(first, last):
                for m, r, k in SPLITS[first:last]:
                    act.wait_ge(raw_sems[max(r // 4 - 2, 0)], 48 if r < R_WNAT else 16)
                    fn(WHI[:, m:m + k, :, :], RAWM[:, r:r + k, :, :], ACT.Copy).then_inc(setup["w_hi"], 1)

            split_hi(0, 1)
            act.wait_ge(setup["w_lo"], 1)
            for h in range(H2):
                act.wait_ge(setup["t1_ps"], h + 1)
                fn(T1[:, h, :, :], PS[:, h, :], ACT.Copy).then_inc(setup["t1_sb"], 1)
            split_hi(1, 4)
            for n in range(H2 + 1):
                act.wait_ge(setup["g_ps"], n + 1)
                m, b = (M_G + n, n) if n < H2 else (M_FG + 1, 5)
                fn(WHI[:, m, :, :], PS[:, b, :], ACT.Copy).then_inc(setup["g_hi"], 1)
            split_hi(4, len(SPLITS))

            def h_hi(s, c, halves):
                act.wait_ge(S[s]["hT_ps"], halves[c])
                fn(HT[s][:, 0, c, :], bank(s, H_BANKS[c])[:, 0:TOK], ACT.Relu).then_inc(S[s]["hT_hi"], 1)

            def att(s, k, a, i, v):
                sm, n = S[s], v.att[a]
                if k == "turn":
                    h_hi(s, i, norm_halves(a, v))
                elif k == "q":
                    act.wait_ge(sm["q_ps"], n)
                    if a == 0:
                        for oc in range(DC):
                            last = fn(Q[s][:, oc, :], bank(s, 1)[:, oc * TOK:oc * TOK + TOK], ACT.Identity,
                                      bias=COLS[:, oc:oc + 1])
                    else:
                        last = fn(Q[s][:, :, :], bank(s, 1), ACT.Copy)
                    last.then_inc(sm["q_sb"], 1)
                elif k == "v":
                    act.wait_ge(sm["v_ps"], n)
                    fn(V[s][:, :, :], bank(s, 3), ACT.Copy).then_inc(sm["v_sb"], 1)
                elif k == "max":
                    u, m, j, cj = i
                    act.wait_ge(sm["rowmax"], v.eight[u])
                    for b in range(NB):
                        at, row = (cj * NB + b) * SQ, m * NB + b
                        p = PR[s][:, j, at:at + SQ]
                        last = fn(p, p, ACT.Exp, bias=ROWMAX[s][:, row:row + 1], accum_out=ROWSUM[s][:, row:row + 1])
                    last.then_inc(sm["exp"], 1)
                elif k == "pt":
                    act.wait_ge(sm["pt_ps"], v.six[2 * a + i])
                    us = turned(a)[i]
                    _, _, j, cj = us[0]
                    at = slice(cj * TOK, (cj + len(us)) * TOK)
                    fn(PTS[s][:, j, at], bank(s, 1 - i)[:, at], ACT.Copy).then_inc(sm["pt_sb"], 1)
                elif k == "pv":
                    act.wait_ge(sm["o_ps"], v.six[2 * a + i])
                    fn(OT[s][:, 0, i, :].rearrange("p (t e q) -> p t e q", t=TT, e=2), o_view(s, i), ACT.Copy
                       ).then_inc(sm["oT_hi"], 1)

            def l2(s, k, i, v):
                sm, n = S[s], v.once
                if k == "turn":
                    h_hi(s, i, norm_halves(L2, v))
                elif k == "h":
                    fn(CT[s][:, 0, :], XN[s][:, :], ACT.Relu).then_inc(sm["hh_ready"], 1)
                elif k == "r":
                    act.wait_ge(sm["r_ps"], n)
                    fn(RS[s][0:RH, 0:TOK], bank(s, 1)[0:RH, 0:TOK], ACT.Identity, bias=S0[:, :]
                       ).then_inc(sm["r_hi"], 1)
                elif k == "e":
                    act.wait_ge(sm["e_ps"], v.four[i])
                    for oc in range(DC):
                        last = fn(e_view(s, 0, oc, i), e_bank(s, E_BANKS[i], oc), ACT.Identity,
                                  bias=CVEC[:, oc, i:i + 1])
                    last.then_inc(sm["e_hi"], 1)
                elif k == "s2":
                    if i == 0:
                        act.wait_ge(sm["hl_ready"], n)
                    act.wait_ge(sm["s2_ps"], v.two[i])
                    fn(tanh_buf(s, i), bank(s, 2 + i), ACT.Tanh).then_inc(sm["tanh"], 1)
                elif k == "a":
                    act.wait_ge(sm["at_f"], v.two[i])
                    fn(AT[s][:, 0, i, :], tanh_buf(s, i), ACT.Copy).then_inc(sm["at_hi"], 1)
                    act.wait_ge(sm["rs_ps"], v.two[i])
                    fn(RS[s][:, i * 512:i * 512 + 512], bank(s, i)[0:SQ, :], ACT.Copy).then_inc(sm["rs_hi"], 1)
                elif k == "ah":
                    for c in range(DC):
                        act.wait_ge(sm["ah_ps"], v.four[2 * i + c])
                        fn(WIDE[s][:, 0, c, i * 512:i * 512 + 512], bank(s, 2 * (1 - i) + c), ACT.Copy
                           ).then_inc(sm["ah_hi"], 1)
                elif k == "hp":
                    act.wait_ge(sm["hp_ps"], v.four[i])
                    if i >= 2:
                        act.wait_ge(sm["ha_mm"], v.four[i - 2])
                    fn(CT[s][:, 0, :] if i % 2 == 0 else AT[s][:, 0, 0, :], bank(s, HEAD_BANKS[i % 2]), ACT.Relu
                       ).then_inc(sm["ct_hi"], 1)
                elif k == "ha" and i == H2 - 1:
                    act.wait_ge(sm["ha_mm"], v.four[i])
                    fn(F[s][:, 0:512], bank(s, 2), ACT.Copy).then_inc(sm["ha_sb"], 1)
                elif k == "hat":
                    act.wait_ge(sm["hat_ps"], v.two[i])
                    at = slice(i * TOK, i * TOK + TOK)
                    fn(CT[s][:, 0, at], bank(s, HAT_BANKS[i])[:, 0:TOK], ACT.Copy).then_inc(sm["hat_hi"], 1)
                elif k == "g":
                    act.wait_ge(sm["g_ps"], v.two[i])
                    fn(XN[s][:, i * D:i * D + D], bank(s, G_BANKS[i])[:, D:2 * D], ACT.Tanh, scale=0.5
                       ).then_inc(sm["gate_t"], 1)

            def step(s, what, v):
                k, a, i = what
                if a == L2:
                    l2(s, k, i, v)
                else:
                    att(s, k, a, i, v)

            passes(act, step, ORDER["act"])

        @block.vector
        def _(dve):
            tt, ts, stt = nc.vector.tensor_tensor, nc.vector.tensor_scalar, nc.vector.scalar_tensor_tensor

            def lo_part(o, full, hi):
                return tt(o, full, hi.bitcast(F32), ALU.subtract)

            dve.wait_ge(setup["rows"], 1)
            tt(RAWR[:, :], RAWR[:, :], RAWRH[:, :].bitcast(F32), ALU.subtract).then_inc(setup["rows"], 1)
            dve.wait_ge(setup["rows"], 2)
            ts(RAWR[:, :], RAWR[:, :], RAWC[0:SQ, C_SELAB + 1:C_SELAB + 2], None, ALU.mult).then_inc(setup["rows"], 1)
            dve.wait_ge(setup["rows"], 3)
            stt(ROWS[:, :], RAWRH[:, :].bitcast(F32), RAWC[0:SQ, C_SELAB:C_SELAB + 1], RAWR[:, :], ALU.mult, ALU.add
                ).then_inc(setup["rows"], 1)
            def split_lo(first, last):
                for n in range(first, last):
                    m, r, k = SPLITS[n]
                    dve.wait_ge(setup["w_hi"], n + 1)
                    lo_part(WLO[:, m:m + k, :, :], RAWM[:, r:r + k, :, :], WHI[:, m:m + k, :, :]
                            ).then_inc(setup["w_lo"], 1)

            split_lo(0, 1)
            dve.wait_ge(setup["zeroed"], 1)
            for part in (0, LO):
                nc.vector.tensor_copy(BPAD[:, :, part:part + H2].rearrange("p c h -> p h c"),
                                      COLS[:, 4:12].rearrange("p (h c) -> p h c", h=H2))
            split_lo(1, 3)
            dve.wait_ge(setup["vec_ps"], 1)
            nc.vector.tensor_copy(A1[:, :, :], PS[:, 4, 0:DC * H2]).then_inc(setup["vec_sb"], 1)
            split_lo(3, 4)
            for n in range(H2 + 1):
                dve.wait_ge(setup["g_hi"], n + 1)
                m, b = (M_G + n, n) if n < H2 else (M_FG + 1, 5)
                lo_part(WLO[:, m, :, :], PS[:, b, :].rearrange("p (c o) -> p c o", c=DC), WHI[:, m, :, :]
                        ).then_inc(setup["g_lo"], 1)
            split_lo(4, len(SPLITS))
            dve.wait_ge(setup["vec_ps"], 2)
            nc.vector.tensor_copy(CVEC[:, :, :], PS[:, 6, 0:DC * H2])
            for part in (0, LO):
                nc.vector.tensor_copy(UPAD[:, :, part:part + H2], PS[:, 7, 0:DC * H2].rearrange("p (c h) -> p c h", c=DC)
                                      ).then_inc(setup["u"], 1)
            dve.wait_ge(setup["u"], 2)
            nc.vector.tensor_copy(UVEC[:, 0, :, :], UPAD[:, :, :]).then_inc(setup["u"], 1)
            dve.wait_ge(setup["u"], 3)
            lo_part(UVEC[:, 1, :, :], UPAD[:, :, :], UVEC[:, 0, :, :])
            tt(S0M[:, :], PS[0:RH, 4, 0:H2], HEADS, ALU.mult).then_inc(setup["vec_sb"], 1)
            dve.wait_ge(setup["vec_sb"], 2)
            nc.vector.reduce_sum(S0[:, :], S0M[:, :], AX_X).then_inc(setup["vec_sb"], 1)
            dve.wait_ge(setup["vec_sb"], 3)

            def x_ready(s, a, t, v):
                sm = S[s]
                if a == L2:
                    dve.wait_ge(sm["res"], v.six[2 + t])
                elif a == 0:
                    dve.wait_ge(sm["x_in"], v.dma)
                elif a == 1:
                    dve.wait_ge(sm["res"], v.six[t])
                else:
                    dve.wait_ge(sm["res2"], v.once)

            def bn(s, a, t, v):
                x_ready(s, a, t, v)
                nc.vector.bn_stats(STATS[s][:, t, :], X[s][:, t * D:t * D + D]).then_inc(S[s]["bn"], 1)

            def stats(s, a, v):
                sm, n = S[s], norm_count(a, v)
                dve.wait_ge(sm["bn"], norm_halves(a, v)[1])
                alone(dve)
                for t in range(TT):
                    last = nc.vector.bn_aggr(MV[s][:, t, :], STATS[s][:, t, :])
                last.then_inc(sm["var"], 1)
                dve.wait_ge(sm["var"], n)
                ts(VE[s], MV[s][:, :, 1], EPS, None, ALU.add).then_inc(sm["ve"], 1)

            def norm(s, a, v, before):
                if a == 0 and before is not None:
                    dve.wait_ge(S[s]["stored"], before)
                dve.wait_ge(S[s]["rstd"], norm_count(a, v))
                for t in range(TT):
                    ts(XN[s][:, t * D:t * D + D], X[s][:, t * D:t * D + D], MV[s][:, t, 0:1],
                       RSTD[s][:, t:t + 1], ALU.subtract, ALU.mult).then_inc(S[s]["xn_ready"], 1)

            def masks(s, v):
                sm = S[s]
                dve.wait_ge(sm["adj_in"], v.dma2)
                ts(MASKA[s][:, :], ADJ8[s][:, :], -1.0, -MASKED, ALU.add, ALU.mult).then_inc(sm["masks"], 1)
                dve.wait_ge(sm["masks"], v.two[0])
                tt(MASKO[s][:, :].rearrange("p (b k) -> p b k", b=NB), MASKA[s][:, :].rearrange("p (b k) -> p b k", b=NB),
                   EYE.unsqueeze(1).broadcast_to([P, NB, SQ]), ALU.max).then_inc(sm["masks"], 1)

            def h_lo(s, c, halves):
                dve.wait_ge(S[s]["hT_hi"], halves[c])
                stt(HT[s][:, 1, c, :], bank(s, H_BANKS[c])[:, 0:TOK], 0.0,
                    HT[s][:, 0, c, :].bitcast(F32), ALU.max, ALU.subtract).then_inc(S[s]["hT_lo"], 1)

            def att(s, k, a, i, v):
                sm, L, n = S[s], ATT[a], v.att[a]
                hd = D // L["heads"]
                two = L["heads"] == 8
                scale = float(hd) ** -0.5
                rows = lambda x: x.rearrange("p (b k) -> p b k", k=SQ)
                if k == "bn":
                    bn(s, a, i, v)
                elif k == "stats":
                    stats(s, a, v)
                elif k == "norm":
                    norm(s, a, v, v.before)
                elif k == "masks":
                    masks(s, v)
                elif k == "turn":
                    h_lo(s, i, norm_halves(a, v))
                elif k == "k":
                    dve.wait_ge(sm["k_ps"], n)
                    if a == 0:
                        for oc in range(DC):
                            last = ts(K[s][:, oc, :], bank(s, 2)[:, oc * TOK:oc * TOK + TOK], COLS[:, 2 + oc:3 + oc],
                                      None, ALU.add)
                    else:
                        last = nc.vector.tensor_copy(K[s][:, :, :], bank(s, 2))
                    last.then_inc(sm["k_sb"], 1)
                elif k == "mask":
                    u, m, j, cj = i
                    at = slice(cj * TOK, cj * TOK + TOK)
                    dve.wait_ge(sm["s_ps"], v.eight[u])
                    if two and m == 3:
                        dve.wait_ge(sm["masks"], v.two[1])
                        mask = rows(MASKO[s][:, :])
                    elif two:
                        mask = STATIC[:, j + 2 * cj:j + 2 * cj + 1, :].broadcast_to([P, NB, SQ])
                    else:
                        mask = rows(MASKA[s][:, :])
                    stt(rows(PR[s][:, j, at]), rows(bank(s, m)[:, 0:TOK]), scale, mask, ALU.mult, ALU.add
                        ).then_inc(sm["masked"], 1)
                elif k == "max":
                    u, m, j, cj = i
                    dve.wait_ge(sm["masked"], v.eight[u])
                    nc.vector.reduce_max(ROWMAX[s][:, m * NB:m * NB + NB], rows(PR[s][:, j, cj * TOK:cj * TOK + TOK]),
                                         AX_X, negate=True).then_inc(sm["rowmax"], 1)
                elif k == "soft":
                    u, m, j, cj = i
                    p = rows(PR[s][:, j, cj * TOK:cj * TOK + TOK])
                    recip = RECIP[s][:, m * NB:m * NB + NB]
                    dve.wait_ge(sm["exp"], v.eight[u])
                    nc.vector.reciprocal(recip, ROWSUM[s][:, m * NB:m * NB + NB]).then_inc(sm["recip"], 1)
                    dve.wait_ge(sm["recip"], v.eight[u])
                    tt(p, p, recip.unsqueeze(2).broadcast_to([P, NB, SQ]), ALU.mult).then_inc(sm["probs"], 1)
                elif k == "pv":
                    dve.wait_ge(sm["oT_hi"], v.six[2 * a + i])
                    order = lambda x: x.rearrange("p (t e q) -> p t e q", t=TT, e=2)
                    lo_part(order(OT[s][:, 1, i, :]), o_view(s, i), order(OT[s][:, 0, i, :])).then_inc(sm["oT_lo"], 1)
                elif k == "out":
                    at = slice(i * D, i * D + D)
                    dve.wait_ge(sm["y_ps"], v.six[2 * a + i])
                    tt((XN if a == 2 else X)[s][:, at], bank(s, Y_BANKS[i])[:, 0:D], X[s][:, at], ALU.add
                       ).then_inc(sm["res"], 1)

            def l2(s, k, i, v):
                sm, n = S[s], v.once
                if k == "bn":
                    bn(s, L2, i, v)
                elif k == "stats":
                    stats(s, L2, v)
                elif k == "norm":
                    norm(s, L2, v, None)
                elif k == "turn":
                    h_lo(s, i, norm_halves(L2, v))
                elif k == "h":
                    dve.wait_ge(sm["hh_ready"], n)
                    stt(CT[s][:, 1, :], XN[s][:, :], 0.0, CT[s][:, 0, :].bitcast(F32), ALU.max, ALU.subtract
                        ).then_inc(sm["hl_ready"], 1)
                elif k == "r":
                    dve.wait_ge(sm["r_hi"], n)
                    stt(RS[s][LO:RH, 0:TOK], bank(s, 1)[LO:RH, 0:TOK], S0[LO:RH, :],
                        RS[s][LO:RH, 0:TOK].bitcast(F32), ALU.add, ALU.subtract).then_inc(sm["r_lo"], 1)
                elif k == "e":
                    dve.wait_ge(sm["e_hi"], v.four[i])
                    for oc in range(DC):
                        stt(e_view(s, 1, oc, i), e_bank(s, E_BANKS[i], oc), CVEC[:, oc, i:i + 1],
                            e_view(s, 0, oc, i).bitcast(F32), ALU.add, ALU.subtract).then_inc(sm["e_lo"], 1)
                elif k == "s2":
                    if i == 0:
                        dve.wait_ge(sm["adjT_in"], v.dma2)
                    dve.wait_ge(sm["tanh"], v.two[i])
                    seen = ADJT8[s][:, i, :, :].unsqueeze(2).broadcast_to([P, 2, H2, SQ])
                    view = tanh_buf(s, i).rearrange("p (e h q) -> p e h q", e=2, h=H2)
                    tt(view, view, seen, ALU.mult).then_inc(sm["at_f"], 1)
                elif k == "a":
                    dve.wait_ge(sm["at_hi"], v.two[i])
                    lo_part(AT[s][:, 1, i, :], tanh_buf(s, i), AT[s][:, 0, i, :]).then_inc(sm["at_lo"], 1)
                    dve.wait_ge(sm["rs_hi"], v.two[i])
                    at = slice(i * 512, i * 512 + 512)
                    lo_part(RS[s][32:SQ, at], bank(s, i)[32:SQ, :], RS[s][32:SQ, at]).then_inc(sm["rs_lo"], 1)
                elif k == "ah":
                    at = slice(i * 512, i * 512 + 512)
                    for c in range(DC):
                        dve.wait_ge(sm["ah_hi"], v.four[2 * i + c])
                        lo_part(WIDE[s][:, 1, c, at], bank(s, 2 * (1 - i) + c), WIDE[s][:, 0, c, at]
                                ).then_inc(sm["ah_lo"], 1)
                elif k == "hp":
                    dve.wait_ge(sm["ct_hi"], v.four[i])
                    hi, lo = ((CT[s][:, 0, :], CT[s][:, 1, :]) if i % 2 == 0 else (AT[s][:, 0, 0, :], AT[s][:, 1, 0, :]))
                    stt(lo, bank(s, HEAD_BANKS[i % 2]), 0.0, hi.bitcast(F32), ALU.max, ALU.subtract).then_inc(sm["ct_lo"], 1)
                elif k == "hat":
                    dve.wait_ge(sm["hat_hi"], v.two[i])
                    at = slice(i * TOK, i * TOK + TOK)
                    lo_part(CT[s][:, 1, at], bank(s, HAT_BANKS[i])[:, 0:TOK], CT[s][:, 0, at]).then_inc(sm["hat_lo"], 1)
                elif k == "g":
                    dve.wait_ge(sm["gate_t"], v.two[i])
                    diff = F[s][:, 512 + i * D:512 + i * D + D]
                    tt(diff, bank(s, G_BANKS[i])[:, 0:D], F[s][:, i * D:i * D + D], ALU.subtract).then_inc(sm["diff"], 1)
                    dve.wait_ge(sm["diff"], v.two[i])
                    stt(diff, XN[s][:, i * D:i * D + D], 1.0, diff, ALU.add, ALU.mult).then_inc(sm["gated"], 1)
                elif k == "sum":
                    dve.wait_ge(sm["x_ha"], n)
                    dve.wait_ge(sm["gated"], v.two[1])
                    stt(X[s][:, :], F[s][:, 512:1024], 0.5, X[s][:, :], ALU.mult, ALU.add).then_inc(sm["res2"], 1)

            def step(s, what, v):
                k, a, i = what
                if a == L2:
                    l2(s, k, i, v)
                else:
                    att(s, k, a, i, v)

            passes(dve, step, ORDER["dve"])


def kernel(**inputs):
    import concourse.bacc as bacc
    from concourse.bass_utils import run_bass_kernel_spmd

    a = {k: np.asarray(v) for k, v in inputs.items()}
    x, adj = a["x"], a["adj"]
    boards = x.shape[0]
    W = a["L2_gnn_W"]
    mats = ([a[f"L0_gnn_W{k}"].T for k in "qkvo"] + [a[f"L{n}_gnn_W{k}"] for n in (1, 3) for k in "qkvo"]
            + list(W) + [w.T for w in W] + [w.T for w in a["L2_gnn_attn"]]
            + list(a["L2_gnn_A_w"].T.reshape(H2, D, D))
            + [a["L2_gnn_fc_w"].T, a["L2_gnn_fc_w"], a["L2_gnn_g1_w"].T, a["L2_gnn_g2_w"].T])
    chunks = lambda b: b.reshape(-1, P).T
    cols = np.concatenate([chunks(a["L0_gnn_bq"]), chunks(a["L0_gnn_bk"]), chunks(a["L2_gnn_bW"])], axis=1)
    rows = np.zeros((SQ, H2 * D), np.float32)
    rows[[0, 1, 32]] = a["L2_gnn_bW"].reshape(-1)
    rows[2:4] = np.concatenate([a["L0_gnn_bv"], a["L0_gnn_bo"], a["L1_gnn_bo"], a["L3_gnn_bo"]])
    rows[4:6, 0:D] = a["L2_gnn_gbias"]
    arrays = {
        "x": x.reshape(-1, D),
        "adjq": adj.transpose(1, 0, 2),
        "adjt": adj.reshape(boards // 2, 2, SQ, SQ).transpose(1, 3, 0, 2),
        "mats": np.stack(mats), "cols": cols, "rows": rows, "board_consts": constants(),
    }
    nc = bacc.Bacc("TRN2", target_bir_lowering=False, num_devices=1)
    arrays = {k: np.ascontiguousarray(v) for k, v in arrays.items()}
    args = [nc.dram_tensor(k, v.shape, mybir.dt.from_np(v.dtype), kind="ExternalInput").ap() for k, v in arrays.items()]
    out = nc.dram_tensor("out", (boards * SQ, D), F32, kind="ExternalOutput").ap()
    build(nc, *args, out)
    r = run_bass_kernel_spmd(nc, [arrays], core_ids=[0])
    return r.results[0]["out"].reshape(boards, SQ, D)
```
